# Optimizing a Trainium2 kernel written in Bass

```python
import numpy as np
import jax
import jax.numpy as jnp

def _softmax(x, axis=-1):
    return jax.nn.softmax(x, axis=axis)

def _gelu(x):
    return jax.nn.gelu(x, approximate=True)

def _silu(x):
    return jax.nn.silu(x)

def _sigmoid(x):
    return jax.nn.sigmoid(x)

def _layernorm(x, axis=-1, eps=1e-05):
    m = jnp.mean(x, axis=axis, keepdims=True)
    v = jnp.var(x, axis=axis, keepdims=True)
    return (x - m) / jnp.sqrt(v + eps)

def _scatter_add(tgt, idx, src, axis=0):
    return tgt.at[idx].add(src)

def _segment_sum(src, seg, n):
    return jax.ops.segment_sum(src, seg, n)
kernel_name = 'mk_audio_tower_d1_tok_aud1d512_r4_948a04'

def setup_inputs(seed: int=0):
    np.random.seed(seed)
    _w = jnp.asarray

    def _rec_inputs():
        import jax
        import jax.numpy as jnp
        _rk = jax.random.key(seed)
        x = -0.00238186 + 1.00146 * jax.random.normal(jax.random.fold_in(_rk, 1), (64, 5000), jnp.float32)
        return x
    x = _rec_inputs()

    def _L0_tok_setup():
        import jax, jax.numpy as jnp
        import numpy as np
        B, E, G, P = (8, 16, 5000, 128)
        MASK_DENSITY = 0.1
        key = jax.random.key(seed)
        k_x, k_w, k_m = jax.random.split(key, 3)
        x = jax.random.normal(k_x, (B, G), dtype=jnp.float32)
        weight = jax.random.normal(k_w, (E, G, P), dtype=jnp.float32) * 0.01
        bias = jnp.zeros((E, P), dtype=jnp.float32)
        mask = (jax.random.uniform(k_m, (G, P)) < MASK_DENSITY).astype(jnp.float32)
        return {'x': x, 'weight': weight, 'bias': bias, 'mask': mask}
    _L0_tok_all = _L0_tok_setup()
    _L0_tok_in = {k: v for k, v in _L0_tok_all.items() if k in ('weight', 'bias', 'mask')}
    del _L0_tok_all

    def _L0_attn_setup():
        import jax, jax.numpy as jnp
        import numpy as np
        B, S, IN, HID, H, D, FF = (8, 512, 128, 128, 8, 64, 512)
        EPS = 1e-05

        def layer_norm(x, g, b):
            m = jnp.mean(x, axis=-1, keepdims=True)
            v = jnp.mean(jnp.square(x - m), axis=-1, keepdims=True)
            return (x - m) * jax.lax.rsqrt(v + EPS) * g + b

        def delta_rule(q, k, v, beta):

            def step(W, inp):
                qt, kt, vt, bt = inp
                wk = jnp.einsum('bhde,bhe->bhd', W, kt)
                v_new = bt * (vt - wk)
                W = W + jnp.einsum('bhd,bhe->bhde', v_new, kt)
                out = jnp.einsum('bhde,bhe->bhd', W, qt)
                return (W, out)
            bsz = q.shape[1]
            W0 = jnp.zeros((bsz, H, D, D), dtype=q.dtype)
            _, outs = jax.lax.scan(step, W0, (q, k, v, beta))
            return outs

        def fast_ff(x, ln_g, ln_b, slow_w, out_w):
            slen, bsz, _ = x.shape
            h = layer_norm(x, ln_g, ln_b)
            qkvb = jnp.einsum('sbi,oi->sbo', h, slow_w).reshape(slen, bsz, H, 3 * D + 1)
            q, k, v, beta = jnp.split(qkvb, [D, 2 * D, 3 * D], axis=-1)
            q = jax.nn.softmax(q, axis=-1)
            k = jax.nn.softmax(k, axis=-1)
            beta = jax.nn.sigmoid(beta)
            attn = delta_rule(q, k, v, beta)
            o = jnp.einsum('sbd,od->sbo', attn.reshape(slen, bsz, H * D), out_w)
            return x + o

        def ffn(x, ln_g, ln_b, w1, b1, w2, b2):
            h = layer_norm(x, ln_g, ln_b)
            h = jax.nn.relu(jnp.einsum('sbi,fi->sbf', h, w1) + b1)
            return x + jnp.einsum('sbf,of->sbo', h, w2) + b2
        key = jax.random.key(seed)
        ks = jax.random.split(key, 8)
        s = 0.02
        return {'x': jax.random.normal(ks[0], (B, S, IN), jnp.float32), 'ip_w': s * jax.random.normal(ks[1], (HID, IN), jnp.float32), 'ip_b': jnp.zeros((HID,), jnp.float32), 'fw_ln_g': jnp.ones((2, HID), jnp.float32), 'fw_ln_b': jnp.zeros((2, HID), jnp.float32), 'fw_slow_w': s * jax.random.normal(ks[2], (2, H * (3 * D + 1), HID), jnp.float32), 'fw_out_w': s * jax.random.normal(ks[3], (2, HID, H * D), jnp.float32), 'ff_ln_g': jnp.ones((HID,), jnp.float32), 'ff_ln_b': jnp.zeros((HID,), jnp.float32), 'ff_w1': s * jax.random.normal(ks[4], (FF, HID), jnp.float32), 'ff_b1': jnp.zeros((FF,), jnp.float32), 'ff_w2': s * jax.random.normal(ks[5], (HID, FF), jnp.float32), 'ff_b2': jnp.zeros((HID,), jnp.float32)}
    _L0_attn_all = _L0_attn_setup()
    _L0_attn_in = {k: v for k, v in _L0_attn_all.items() if k in ('ip_w', 'ip_b', 'fw_ln_g', 'fw_ln_b', 'fw_slow_w', 'fw_out_w', 'ff_ln_g', 'ff_ln_b', 'ff_w1', 'ff_b1', 'ff_w2', 'ff_b2')}
    del _L0_attn_all

    def _L0_ffn_setup():
        import jax, jax.numpy as jnp
        import numpy as np
        import math
        D_MODEL = 128
        N_EXPERTS = 128
        TOP_K = 8
        N_HEADS = 8
        D_KEYS = 128
        HALF = D_KEYS // 2
        N_BATCH, T_SEQ = (2, 512)
        key = jax.random.key(seed)
        k1, k2, k3, k4, k5, k6 = jax.random.split(key, 6)
        queries = jax.random.normal(k1, (N_BATCH, T_SEQ, D_MODEL), dtype=jnp.float32)
        bound_q = 1.0 / math.sqrt(D_MODEL)
        Wq = jax.random.uniform(k2, (N_HEADS * D_KEYS, D_MODEL), minval=-bound_q, maxval=bound_q, dtype=jnp.float32)
        bq = jax.random.uniform(k3, (N_HEADS * D_KEYS,), minval=-bound_q, maxval=bound_q, dtype=jnp.float32)
        bound_k = 1.0 / math.sqrt(HALF)
        keys = jax.random.uniform(k4, (N_HEADS, 2, N_EXPERTS, HALF), minval=-bound_k, maxval=bound_k, dtype=jnp.float32)
        std = D_MODEL ** (-0.5)
        w_down_embed = std * jax.random.normal(k5, (N_EXPERTS * N_EXPERTS, D_MODEL), dtype=jnp.float32)
        w_up_embed = std * jax.random.normal(k6, (N_EXPERTS * N_EXPERTS, D_MODEL), dtype=jnp.float32)
        return {'queries': queries, 'Wq': Wq, 'bq': bq, 'keys': keys, 'w_down_embed': w_down_embed, 'w_up_embed': w_up_embed}
    _L0_ffn_all = _L0_ffn_setup()
    _L0_ffn_in = {k: v for k, v in _L0_ffn_all.items() if k in ('Wq', 'bq', 'keys', 'w_down_embed', 'w_up_embed')}
    del _L0_ffn_all
    return {'x': x, 'L0_tok_weight': _L0_tok_in['weight'], 'L0_tok_bias': _L0_tok_in['bias'], 'L0_tok_mask': _L0_tok_in['mask'], 'L0_attn_ip_w': _L0_attn_in['ip_w'], 'L0_attn_ip_b': _L0_attn_in['ip_b'], 'L0_attn_fw_ln_g': _L0_attn_in['fw_ln_g'], 'L0_attn_fw_ln_b': _L0_attn_in['fw_ln_b'], 'L0_attn_fw_slow_w': _L0_attn_in['fw_slow_w'], 'L0_attn_fw_out_w': _L0_attn_in['fw_out_w'], 'L0_attn_ff_ln_g': _L0_attn_in['ff_ln_g'], 'L0_attn_ff_ln_b': _L0_attn_in['ff_ln_b'], 'L0_attn_ff_w1': _L0_attn_in['ff_w1'], 'L0_attn_ff_b1': _L0_attn_in['ff_b1'], 'L0_attn_ff_w2': _L0_attn_in['ff_w2'], 'L0_attn_ff_b2': _L0_attn_in['ff_b2'], 'L0_ffn_Wq': _L0_ffn_in['Wq'], 'L0_ffn_bq': _L0_ffn_in['bq'], 'L0_ffn_keys': _L0_ffn_in['keys'], 'L0_ffn_w_down_embed': _L0_ffn_in['w_down_embed'], 'L0_ffn_w_up_embed': _L0_ffn_in['w_up_embed']}

def reference(x, L0_tok_weight, L0_tok_bias, L0_tok_mask, L0_attn_ip_w, L0_attn_ip_b, L0_attn_fw_ln_g, L0_attn_fw_ln_b, L0_attn_fw_slow_w, L0_attn_fw_out_w, L0_attn_ff_ln_g, L0_attn_ff_ln_b, L0_attn_ff_w1, L0_attn_ff_b1, L0_attn_ff_w2, L0_attn_ff_b2, L0_ffn_Wq, L0_ffn_bq, L0_ffn_keys, L0_ffn_w_down_embed, L0_ffn_w_up_embed):
    import jax
    import jax.numpy as jnp

    def _L0_tok_ref(x, weight, bias, mask):
        import jax, jax.numpy as jnp
        import numpy as np
        B, E, G, P = (8, 16, 5000, 128)
        MASK_DENSITY = 0.1
        W = weight * mask[None, :, :]
        out = jnp.einsum('bg,egp->bep', x, W)
        return out + bias[None, :, :]

    def _L0_attn_ref(x, ip_w, ip_b, fw_ln_g, fw_ln_b, fw_slow_w, fw_out_w, ff_ln_g, ff_ln_b, ff_w1, ff_b1, ff_w2, ff_b2):
        import jax, jax.numpy as jnp
        import numpy as np
        B, S, IN, HID, H, D, FF = (8, 512, 128, 128, 8, 64, 512)
        EPS = 1e-05

        def layer_norm(x, g, b):
            m = jnp.mean(x, axis=-1, keepdims=True)
            v = jnp.mean(jnp.square(x - m), axis=-1, keepdims=True)
            return (x - m) * jax.lax.rsqrt(v + EPS) * g + b

        def delta_rule(q, k, v, beta):

            def step(W, inp):
                qt, kt, vt, bt = inp
                wk = jnp.einsum('bhde,bhe->bhd', W, kt)
                v_new = bt * (vt - wk)
                W = W + jnp.einsum('bhd,bhe->bhde', v_new, kt)
                out = jnp.einsum('bhde,bhe->bhd', W, qt)
                return (W, out)
            bsz = q.shape[1]
            W0 = jnp.zeros((bsz, H, D, D), dtype=q.dtype)
            _, outs = jax.lax.scan(step, W0, (q, k, v, beta))
            return outs

        def fast_ff(x, ln_g, ln_b, slow_w, out_w):
            slen, bsz, _ = x.shape
            h = layer_norm(x, ln_g, ln_b)
            qkvb = jnp.einsum('sbi,oi->sbo', h, slow_w).reshape(slen, bsz, H, 3 * D + 1)
            q, k, v, beta = jnp.split(qkvb, [D, 2 * D, 3 * D], axis=-1)
            q = jax.nn.softmax(q, axis=-1)
            k = jax.nn.softmax(k, axis=-1)
            beta = jax.nn.sigmoid(beta)
            attn = delta_rule(q, k, v, beta)
            o = jnp.einsum('sbd,od->sbo', attn.reshape(slen, bsz, H * D), out_w)
            return x + o

        def ffn(x, ln_g, ln_b, w1, b1, w2, b2):
            h = layer_norm(x, ln_g, ln_b)
            h = jax.nn.relu(jnp.einsum('sbi,fi->sbf', h, w1) + b1)
            return x + jnp.einsum('sbf,of->sbo', h, w2) + b2
        out = jnp.einsum('bsi,hi->bsh', x, ip_w) + ip_b
        out = out.transpose(1, 0, 2)
        out = fast_ff(out, fw_ln_g[0], fw_ln_b[0], fw_slow_w[0], fw_out_w[0])
        out = ffn(out, ff_ln_g, ff_ln_b, ff_w1, ff_b1, ff_w2, ff_b2)
        out = fast_ff(out, fw_ln_g[1], fw_ln_b[1], fw_slow_w[1], fw_out_w[1])
        return out.transpose(1, 0, 2)

    def _L0_ffn_ref(queries, Wq, bq, keys, w_down_embed, w_up_embed):
        import jax, jax.numpy as jnp
        import numpy as np
        import math
        D_MODEL = 128
        N_EXPERTS = 128
        TOP_K = 8
        N_HEADS = 8
        D_KEYS = 128
        HALF = D_KEYS // 2
        N_BATCH, T_SEQ = (2, 512)
        N, T, D = queries.shape
        H, E, K = (N_HEADS, N_EXPERTS, TOP_K)
        q_tok = queries.reshape(-1, D)
        qh = q_tok @ Wq.T + bq
        qh = qh.reshape(-1, H, 2, HALF)
        sub_scores = jnp.einsum('nhcf,hcef->nhce', qh, keys)
        s, idx = jax.lax.top_k(sub_scores, K)
        all_scores = (s[:, :, 0, :, None] + s[:, :, 1, None, :]).reshape(-1, H, K * K)
        all_idx = (idx[:, :, 0, :, None] * E + idx[:, :, 1, None, :]).reshape(-1, H, K * K)
        best_s, best_pos = jax.lax.top_k(all_scores, K)
        indices = jnp.take_along_axis(all_idx, best_pos, axis=-1)
        w_down = w_down_embed[indices]
        w_up = w_up_embed[indices]
        x = jnp.einsum('nd,nhkd->nhk', q_tok, w_down)
        x = jax.nn.gelu(x)
        vals = x * jax.nn.softmax(best_s, axis=-1)
        out = jnp.einsum('nhk,nhkd->nd', vals, w_up)
        return out.reshape(N, T, D)
    h = _L0_tok_ref(x, L0_tok_weight, L0_tok_bias, L0_tok_mask)
    h = h + _L0_attn_ref(_layernorm(h, axis=-1), L0_attn_ip_w, L0_attn_ip_b, L0_attn_fw_ln_g, L0_attn_fw_ln_b, L0_attn_fw_slow_w, L0_attn_fw_out_w, L0_attn_ff_ln_g, L0_attn_ff_ln_b, L0_attn_ff_w1, L0_attn_ff_b1, L0_attn_ff_w2, L0_attn_ff_b2)
    h = h + _L0_ffn_ref(_layernorm(h, axis=-1), L0_ffn_Wq, L0_ffn_bq, L0_ffn_keys, L0_ffn_w_down_embed, L0_ffn_w_up_embed)
    return h

_drawn_inputs = setup_inputs


def setup_inputs(seed=0):
    import zlib

    import numpy as np

    out = dict(_drawn_inputs(seed))
    spreads = {'L0_tok_bias': (0.0, 0.1),
     'L0_attn_ip_b': (0.0, 0.1),
     'L0_attn_fw_ln_g': (1.0, 0.6),
     'L0_attn_fw_ln_b': (0.0, 0.577),
     'L0_attn_ff_ln_g': (1.0, 0.2),
     'L0_attn_ff_ln_b': (0.0, 0.1),
     'L0_attn_ff_b1': (0.0, 0.1),
     'L0_attn_ff_b2': (0.0, 0.1)}
    factors = {}
    for name, (base, spread) in spreads.items():
        noise = np.random.default_rng([zlib.crc32(name.encode()), seed]).standard_normal(out[name].shape)
        drawn = base * np.exp(spread * noise) if base else spread * noise
        out[name] = jnp.asarray(drawn.astype(out[name].dtype))
    for name, factor in factors.items():
        out[name] = (out[name] * factor).astype(out[name].dtype)
    return out
```

```python
from contextlib import ExitStack

import numpy as np
import concourse.bass as bass
from concourse import mybir

F32 = mybir.dt.float32
U32 = mybir.dt.uint32
I32 = mybir.dt.int32
ALU = mybir.AluOpType
ACT = mybir.ActivationFunctionType
AX = mybir.AxisListType

B, G = 64, 5000
S, P = 16, 128
H, D = 8, 64
HP = H // 2
FC = 4
K = 8
SLOTS = H * K
TILES = B * S // P
GP = 125
GC = G // GP
CG = 4
WG = GC // CG
RING = 4
EPS = 1e-5

QKV = 3 * H * D + H
OFF = {}
_at = 0
for _name, _n in (("ip", P), ("slow0", QKV), ("slow1", QKV), ("out0", HP * P), ("out1", HP * P),
                  ("w1", FC * P), ("w2", FC * P), ("wq", H * P), ("keys", H * P),
                  ("g0", 1), ("b0", 1), ("g1", 1), ("b1", 1), ("gf", 1), ("bf", 1), ("fb1", FC), ("bq", H)):
    OFF[_name] = _at
    _at += _n
PACKED = _at

(P_U, P_L, P_S, P_A2, P_T4, P_T4T, P_A4, P_T8T, P_Y, P_W, P_Z) = range(1, 12)
PRODUCTS = 11
(V_T2T, V_U8, V_T2, V_S, V_A2, V_A4, V_R) = range(1, 8)
MOVED_V = 7
(C_U, C_T4, C_T4T, C_T8T, C_Y, C_Z) = range(1, 7)
MOVED_C = 6
NORMS = 5
CHUNKS = 4
CS = SLOTS // CHUNKS


def build(nc, weight, x_t, mask, packed, bias, rows, fconst, iconst, table, h_dram, out):
    with ExitStack() as ctx:
        def sb(name, shape, dt=F32):
            return ctx.enter_context(nc.sbuf_tensor(name, shape, dt))

        def sem(name):
            return ctx.enter_context(nc.semaphore(name))

        mats = sb("mats", [P, PACKED])
        bias_sb = sb("bias_sb", [P, P])
        rows_sb = sb("rows_sb", [P, 2 * P])
        fc_sb = sb("fc_sb", [P, 3 * P + K])
        ic_sb = sb("ic_sb", [P, 4 * P], I32)
        mask_mem = sb("mask_mem", [P, GC * P])
        x_mem = sb("x_mem", [P, GC * B])
        mask_sb, x_sb = mask_mem[0:GP, :], x_mem[0:GP, :]
        ring = sb("ring", [P, RING, S // 2 * CG * P])
        rows_got = ring[:, :, :].rearrange("p r (s n) -> p (r s) n", n=2 * P)
        h_cols = sb("h_cols", [P, 2, 512])
        h_tok = sb("h_tok", [P, TILES, P])
        ident = fc_sb[:, 0:P]
        mask_u8 = fc_sb[:, P:2 * P]
        mask_s = fc_sb[:, 2 * P:3 * P]
        iota8 = fc_sb[:, 3 * P:3 * P + K]
        m1, m1t, m2, m4 = (ic_sb[:, P * n:P * (n + 1)] for n in range(4))

        def mat(name, n, w=P):
            return mats[:, OFF[name] + n * w:OFF[name] + (n + 1) * w]

        stats = sb("stats", [P, 6])
        mv = sb("mv", [P, 2])
        var = sb("var", [P, 1])
        rs = sb("rs", [P, 1])
        rs2 = sb("rs2", [P, 1])
        normed = sb("normed", [P, P])
        normed_t = sb("normed_t", [P, P])
        h0 = sb("h0", [P, P])
        xs = sb("xs", [P, P])
        xs2 = sb("xs2", [P, P])
        ff = x_mem[:, (H + HP) * P:(H + HP + FC) * P].rearrange("p (n q) -> p n q", n=FC)
        nmax = sb("nmax", [P, 2 * H])
        esum = sb("esum", [P, 2 * H])
        rsum = sb("rsum", [P, 2 * H])
        tb = sb("tb", [P, H])
        beta = sb("beta", [P, H])
        rb = sb("rb", [P, H])
        rrb = sb("rrb", [P, H])
        eqk = sb("eqk", [P, 2 * H, D])
        ekc = sb("ekc", [P, H, D])
        rhs_v = sb("rhs_v", [P, H, D])
        eq_t = sb("eq_t", [P, HP, P])
        ek_t = sb("ek_t", [P, HP, P])
        ekc_t = sb("ekc_t", [P, HP, P])

        def halves(name, width=P):
            return [sb(f"{name}{f}", [P, HP, width]) for f in range(2)]

        u_raw, u8, s_m = halves("u_raw"), halves("u8"), halves("s_m")
        t2, t2t, a2, a4 = halves("t2_"), halves("t2t_"), halves("a2_"), halves("a4_")
        t4, t4t, t8t = halves("t4_"), halves("t4t_"), halves("t8t_")
        y, r2, z = halves("y", D), halves("r2_", D), halves("z", D)
        o_t = x_mem[:, H * P:H * P + HP * P].rearrange("p (i q) -> p i q", i=HP)
        qh_t = x_mem[:, 0:H * P].rearrange("p (h q) -> p h q", h=H)
        best = sb("best", [P, 2, H, K])
        besti = sb("besti", [P, 2, H, K], U32)
        bestf = sb("bestf", [P, 2, H, K])
        top = sb("top", [P, H, K])
        topi = sb("topi", [P, H, K], U32)
        pos = sb("pos", [P, 2, SLOTS], U32)
        posf = sb("posf", [P, 2, SLOTS])
        half_i = sb("half_i", [P, 2, SLOTS])
        shifted = sb("shifted", [P, H, K])
        w_exp = sb("w_exp", [P, H, K])
        w_sum = sb("w_sum", [P, H])
        w_rec = sb("w_rec", [P, H])
        w_next = sb("w_next", [P, SLOTS])
        idx_next = sb("idx_next", [P, SLOTS], U32)
        w_now = sb("w_now", [P, SLOTS])
        idx_now = sb("idx_now", [P, SLOTS], U32)
        q_now = sb("q_now", [P, P])
        h_now = sb("h_now", [P, P])
        prod = mask_mem[:, 0:CS * P].rearrange("p (s q) -> p s q", s=CS)
        xd = sb("xd", [P, CS])
        g1, g2 = sb("g1_", [P, CS]), sb("g2_", [P, CS])
        g3, g4 = sb("g3_", [P, CS]), sb("g4_", [P, CS])
        th = sb("th", [P, CS])
        val = sb("val", [P, CS])
        diag = mask_mem[:, CS * P:2 * CS * P].rearrange("p (s q) -> p s q", s=CS)
        cand = mask_mem[:, 2 * CS * P:2 * CS * P + H * K * K].rearrange("p (h a b) -> p h a b", h=H, a=K)
        hot = mask_mem[:, 2 * CS * P + H * K * K:2 * CS * P + 2 * H * K * K].rearrange("p (s a) -> p s a", a=K)

        ps = ctx.enter_context(nc.psum_tensor("ps", [P, 8 * 512], F32))

        def bank(n, lo=0, hi=512):
            return ps[:, 512 * n + lo:512 * n + hi]

        SOLVE = ((4, 5, 6), (0, 1, 3))
        UP = 7

        w_landed = [sem(f"w_landed{n}") for n in range(RING)]
        x_landed, mask_landed, mats_landed = sem("x_landed"), sem("mask_landed"), sem("mats_landed")
        consts_landed = sem("consts_landed")
        masked, w_used, h_summed, h_copied = sem("masked"), sem("w_used"), sem("h_summed"), sem("h_copied")
        h_stored, h_loaded = sem("h_stored"), sem("h_loaded")
        v_done = sem("v_done")
        c_done = sem("c_done")
        setup_done = sem("setup_done")
        norm_ready, norm_turned, norm_moved = sem("norm_ready"), sem("norm_turned"), sem("norm_moved")
        proj_ready = sem("proj_ready")
        qk_ready, v_ready, nmax_ready = sem("qk_ready"), sem("v_ready"), sem("nmax_ready")
        tb_ready, e_ready, eq_ready, ekc_ready = sem("tb_ready"), sem("e_ready"), sem("eq_ready"), sem("ekc_ready")
        ek_turned, eq_turned, ekc_turned = sem("ek_turned"), sem("eq_turned"), sem("ekc_turned")
        ek_moved, eq_moved, ekc_moved = sem("ek_moved"), sem("eq_moved"), sem("ekc_moved")
        product = [sem(f"product{f}") for f in range(2)]
        moved_v = [sem(f"moved_v{f}") for f in range(2)]
        moved_c = [sem(f"moved_c{f}") for f in range(2)]
        rhs_ready = sem("rhs_ready")
        o_ready, o_moved, att_ready = sem("o_ready"), sem("o_moved"), sem("att_ready")
        ff1_ready, ff1_moved, ff2_ready = sem("ff1_ready"), sem("ff1_moved"), sem("ff2_ready")
        qh_ready, qh_moved, scores_ready = sem("qh_ready"), sem("qh_moved"), sem("scores_ready")
        top_shifted, top_exped, idx_ready = sem("top_shifted"), sem("top_exped"), sem("idx_ready")
        got = [sem(f"got{n}") for n in range(CHUNKS)]
        u_ready, th_ready, val_ready, diag_ready, up_done = (sem("u_ready"), sem("th_ready"), sem("val_ready"),
                                                             sem("diag_ready"), sem("up_done"))
        out_ready, out_stored = sem("out_ready"), sem("out_stored")

        def at(t, a_tile, n):
            return t * a_tile + n

        def al(t, l, a_layer, n):
            return t * (2 * a_layer) + (l * a_layer + n)

        block = ctx.enter_context(nc.Block())

        @block.sync
        def _(sp):
            sp.dma_start(x_sb[:, :], x_t).then_inc(x_landed, 16)
            w_view = weight.rearrange("e (p c) q -> p e (c q)", p=GP)
            for n in range(2 * WG):
                grp, half = n // 2, n % 2
                if n == 1:
                    sp.dma_start(mask_sb[:, :], mask.rearrange("(p c) q -> p (c q)", p=GP)).then_inc(mask_landed, 16)
                if n >= RING:
                    sp.wait_ge(w_used, n - RING + 1)
                sp.dma_start(ring[0:GP, n % RING, :].rearrange("p (e k) -> p e k", e=S // 2),
                             w_view[:, S // 2 * half:S // 2 * (half + 1), CG * P * grp:CG * P * (grp + 1)]
                             ).then_inc(w_landed[n % RING], 16)
            h_view = h_dram.rearrange("b (f j i) q -> j b f (i q)", f=2, j=2)
            sp.wait_ge(h_copied, 2)
            for j in range(2):
                sp.dma_start(h_view[j], h_cols[B * j:B * (j + 1), :, :]).then_inc(h_stored, 16)
            sp.wait_ge(h_stored, 32)
            sp.dma_start(h_tok[:, :, :], h_dram.rearrange("(t a) e q -> (a e) t q", t=TILES)).then_inc(h_loaded, 16)
            out_view = out.rearrange("(t a) e q -> t (a e) q", t=TILES)
            with sp.Fori(0, TILES) as t:
                sp.wait_ge(out_ready, t + 1)
                sp.dma_start(out_view[bass.ds(t, 1), :, :].rearrange("t p q -> p (t q)"),
                             h_tok[:, bass.ds(t, 1), :].rearrange("p t q -> p (t q)")).then_inc(out_stored, 16)
            sp.wait_ge(out_stored, 16 * TILES)

        @block.gpsimd
        def _(pool):
            def gather(t, first):
                pool.wait_ge(idx_ready, t + 1)
                for c in range(CHUNKS):
                    if not first:
                        pool.wait_ge(up_done, at(t, CHUNKS, c + 1 - CHUNKS))
                    pool.nop(nofuse=True)
                    for s in range(CS * c, CS * (c + 1)):
                        pool.indirect_dma_start(
                            out=rows_got[:, s, :], out_offset=None, in_=table,
                            in_offset=bass.IndirectOffsetOnAxis(ap=idx_now[:, s:s + 1], axis=0)
                        ).then_inc(got[c], 16)

            gather(0, True)
            with pool.Fori(1, TILES) as t:
                gather(t, False)

        @block.scalar
        def _(act):
            act.dma_start(fc_sb[:, :], fconst).then_inc(consts_landed, 16)
            act.dma_start(ic_sb[:, :], iconst).then_inc(consts_landed, 16)
            for n in range(P // S):
                act.dma_start(bias_sb[S * n:S * (n + 1), :], bias).then_inc(consts_landed, 16)
            act.dma_start(rows_sb[:, :], rows.partition_broadcast(P)).then_inc(consts_landed, 16)
            act.dma_start(mats[:, :], packed).then_inc(mats_landed, 16)
            act.wait_ge(consts_landed, 16 * (3 + P // S))
            act.wait_ge(mats_landed, 16)
            for f in range(2):
                act.wait_ge(h_summed, f + 1)
                nc.scalar.activation(h_cols[:, f, :], bank(f), ACT.Copy).then_inc(h_copied, 1)

            def move_norm(t, n, g=None, b=None):
                act.wait_ge(norm_turned, at(t, NORMS, n + 1))
                if g is None:
                    nc.scalar.activation(normed_t[:, :], bank(6, 0, P), ACT.Copy).then_inc(norm_moved, 1)
                else:
                    nc.scalar.activation(normed_t[:, :], bank(6, 0, P), ACT.Identity,
                                         bias=mat(b, 0, 1), scale=mat(g, 0, 1)).then_inc(norm_moved, 1)

            def layer_start(t, l):
                act.wait_ge(v_ready, al(t, l, 1, 1))
                nc.scalar.activation(tb[:, :], bank(3, 0, H), ACT.Tanh, scale=0.5).then_inc(tb_ready, 1)
                act.wait_ge(nmax_ready, al(t, l, 1, 1))
                for j in (*range(H, 2 * H), *range(H)):
                    nc.scalar.activation(eqk[:, j, :], ps[:, D * j:D * (j + 1)], ACT.Exp, bias=nmax[:, j:j + 1],
                                         accum_out=esum[:, j:j + 1]).then_inc(e_ready, 1)
                act.wait_ge(ek_turned, al(t, l, 1, 1))
                nc.scalar.activation(ek_t[:, :, :], bank(1), ACT.Copy).then_inc(ek_moved, 1)
                act.wait_ge(eq_turned, al(t, l, 1, 1))
                nc.scalar.activation(eq_t[:, :, :], bank(0), ACT.Copy).then_inc(eq_moved, 1)

            def layer_solve(t, l):
                def move(f, p, dst, src):
                    act.wait_ge(product[f], al(t, l, PRODUCTS, p))
                    nc.scalar.activation(dst[f][:, :, :], src, ACT.Copy).then_inc(moved_c[f], 1)

                for f in range(2):
                    move(f, P_U, u_raw, bank(SOLVE[f][0]))
                for f in range(2):
                    move(f, P_T4, t4, bank(SOLVE[f][0]))
                    move(f, P_T4T, t4t, bank(SOLVE[f][1]))
                for f in range(2):
                    move(f, P_T8T, t8t, bank(SOLVE[f][1]))
                for f in range(2):
                    move(f, P_Y, y, bank(SOLVE[f][0], 0, HP * D))
                for f in range(2):
                    move(f, P_Z, z, bank(SOLVE[f][0], 0, HP * D))

            def feed_forward(t):
                act.wait_ge(ff1_ready, t + 1)
                for n in range(FC):
                    nc.scalar.activation(ff[:, n, :], bank(0, P * n, P * (n + 1)), ACT.Relu,
                                         bias=mat("fb1", n, 1)).then_inc(ff1_moved, 1)

            def routing(t):
                act.wait_ge(qh_ready, t + 1)
                for h in range(H):
                    nc.scalar.activation(qh_t[:, h, :], ps[:, 4 * 512 + P * h:4 * 512 + P * (h + 1)], ACT.Identity,
                                         bias=mat("bq", h, 1)).then_inc(qh_moved, 1)
                act.wait_ge(top_shifted, t + 1)
                nc.scalar.activation(w_exp[:, :, :], shifted[:, :, :], ACT.Exp).then_inc(top_exped, 1)

            def combine(t, c):
                act.wait_ge(u_ready, at(t, CHUNKS, c + 1))
                nc.scalar.activation(th[:, :], g3[:, :], ACT.Tanh, scale=0.7978845608028654).then_inc(th_ready, 1)
                act.wait_ge(val_ready, at(t, CHUNKS, c + 1))
                if c >= 1:
                    act.wait_ge(up_done, at(t, CHUNKS, c))
                for k in range(CS):
                    last = nc.scalar.activation(diag[:, k, :], ident, ACT.Copy, scale=val[:, k:k + 1])
                last.then_inc(diag_ready, 1)

            def attend(t, chunk):
                move_norm(t, 0)
                move_norm(t, 1, "g0", "b0")
                layer_start(t, 0)
                chunk(0)
                layer_solve(t, 0)
                chunk(1)
                move_norm(t, 2, "gf", "bf")
                feed_forward(t)
                move_norm(t, 3, "g1", "b1")
                layer_start(t, 1)
                chunk(2)
                layer_solve(t, 1)
                move_norm(t, 4)
                routing(t)
                chunk(3)

            attend(0, lambda c: None)
            with act.Fori(1, TILES) as t:
                attend(t, lambda c: combine(t - 1, c))
            for c in range(CHUNKS):
                combine(TILES - 1, c)

        @block.vector
        def _(dve):
            v = nc.vector
            count = {v_done: 0, c_done: 0}
            a_tile = {v_done: 0, c_done: 0}

            def did(instruction, s=v_done):
                count[s] += 1
                return instruction.then_inc(s, 1)

            def settle(t, s=v_done, alone=False):
                dve.wait_ge(s, at(t, a_tile[s], count[s]))
                if alone:
                    dve.nop(nofuse=True)

            def hold():
                dve.nop(nofuse=True)

            dve.wait_ge(consts_landed, 16 * (3 + P // S))
            for dst in (*t2, *t2t, *a2, *a4):
                v.tensor_copy(dst[:, :, :], ident.unsqueeze(1).broadcast_to([P, HP, P])).then_inc(setup_done, 1)

            dve.wait_ge(mask_landed, 16)
            for n in range(2 * WG):
                grp = n // 2
                w = ring[0:GP, n % RING, :].rearrange("p (e k) -> p e k", e=S // 2)
                m = mask_sb[:, CG * P * grp:CG * P * (grp + 1)]
                dve.wait_ge(w_landed[n % RING], 16 * (n // RING + 1))
                v.tensor_tensor(w, w, m.unsqueeze(1).broadcast_to([GP, S // 2, CG * P]), ALU.mult).then_inc(masked, 1)
            dve.wait_ge(setup_done, 8)
            dve.wait_ge(h_loaded, 16)
            dve.wait_ge(mats_landed, 16)

            def layer_norm(t, src):
                did(v.bn_stats(stats[:, :], src))
                settle(t, alone=True)
                did(v.bn_aggr(mv[:, :], stats[:, :]))
                settle(t)
                did(v.tensor_scalar(var[:, :], mv[:, 1:2], EPS, None, ALU.add))
                settle(t)
                did(v.tensor_scalar(rs2[:, :].bitcast(I32), var[:, :].bitcast(I32), 1, None, ALU.arith_shift_right))
                settle(t)
                did(v.tensor_scalar(rs[:, :].bitcast(I32), rs2[:, :].bitcast(I32), -1.0, float(0x5F3759DF),
                                    ALU.mult, ALU.add))
                settle(t)
                for _ in range(4):
                    did(v.scalar_tensor_tensor(rs2[:, :], rs[:, :], var[:, :], rs[:, :], ALU.mult, ALU.mult))
                    settle(t)
                    did(v.tensor_scalar(rs2[:, :], rs2[:, :], -0.5, 1.5, ALU.mult, ALU.add))
                    settle(t)
                    did(v.tensor_tensor(rs[:, :], rs[:, :], rs2[:, :], ALU.mult))
                    settle(t)
                v.tensor_scalar(normed[:, :], src, mv[:, 0:1], rs[:, :], ALU.subtract, ALU.mult).then_inc(norm_ready, 1)

            def layer_start(t, l):
                dve.wait_ge(qk_ready, al(t, l, 1, 1))
                v.tensor_reduce(nmax[:, :], ps[:, 0:2 * H * D].rearrange("p (j d) -> p j d", d=D), AX.X, ALU.max,
                                negate=True).then_inc(nmax_ready, 1)
                dve.wait_ge(tb_ready, al(t, l, 1, 1))
                did(v.tensor_scalar(beta[:, :], tb[:, :], 0.5, 0.5, ALU.mult, ALU.add))
                dve.wait_ge(e_ready, al(t, l, 2 * H, H))
                did(v.reciprocal(rsum[:, H:2 * H], esum[:, H:2 * H]))
                settle(t)
                did(v.tensor_tensor(rb[:, :], beta[:, :], rsum[:, H:2 * H], ALU.mult))
                settle(t)
                did(v.scalar_tensor_tensor(rrb[:, :], rb[:, :], -1.0, rsum[:, H:2 * H], ALU.mult, ALU.mult))
                settle(t)
                v.tensor_tensor(ekc[:, :, :], eqk[:, H:2 * H, :], rrb[:, :].unsqueeze(2).broadcast_to([P, H, D]),
                                    ALU.mult).then_inc(ekc_ready, 1)
                dve.wait_ge(e_ready, al(t, l, 2 * H, 2 * H))
                did(v.reciprocal(rsum[:, 0:H], esum[:, 0:H]))
                settle(t)
                v.tensor_tensor(eqk[:, 0:H, :], eqk[:, 0:H, :], rsum[:, 0:H].unsqueeze(2).broadcast_to([P, H, D]),
                                    ALU.mult).then_inc(eq_ready, 1)
                dve.wait_ge(v_ready, al(t, l, 1, 1))
                v.tensor_tensor(rhs_v[:, :, :], bank(2).rearrange("p (h d) -> p h d", d=D),
                                    rb[:, :].unsqueeze(2).broadcast_to([P, H, D]), ALU.mult).then_inc(rhs_ready, 1)
                dve.wait_ge(ekc_turned, al(t, l, 1, 1))
                v.tensor_copy(ekc_t[:, :, :], bank(3)).then_inc(ekc_moved, 1)

            def layer_solve(t, l):
                def masks(m):
                    return m.unsqueeze(1).broadcast_to([P, HP, P])

                def four(f, n):
                    return bank(SOLVE[f][n]).rearrange("p (i q) -> p i q", i=HP)

                def ready(f, p):
                    dve.wait_ge(product[f], al(t, l, PRODUCTS, p))

                for f in range(2):
                    dve.wait_ge(moved_c[f], al(t, l, MOVED_C, C_U))
                    hold()
                    v.copy_predicated(t2t[f][:, :, :], masks(m1t), four(f, 0)).then_inc(moved_v[f], 1)
                    v.tensor_tensor(u8[f][:, :, :], four(f, 0), masks(mask_u8), ALU.mult).then_inc(moved_v[f], 1)
                for f in range(2):
                    ready(f, P_L)
                    hold()
                    v.copy_predicated(t2[f][:, :, :], masks(m1), four(f, 1)).then_inc(moved_v[f], 1)
                for f in range(2):
                    ready(f, P_S)
                    v.tensor_tensor(s_m[f][:, :, :], four(f, 2), masks(mask_s), ALU.mult).then_inc(moved_v[f], 1)
                for f in range(2):
                    ready(f, P_A2)
                    hold()
                    v.copy_predicated(a2[f][:, :, :], masks(m2), four(f, 1)).then_inc(moved_v[f], 1)
                for f in range(2):
                    ready(f, P_A4)
                    hold()
                    v.copy_predicated(a4[f][:, :, :], masks(m4), four(f, 0)).then_inc(moved_v[f], 1)
                for f in range(2):
                    ready(f, P_W)
                    v.tensor_tensor(r2[f][:, :, :], bank(SOLVE[f][1], 0, HP * D).rearrange("p (i d) -> p i d", d=D),
                                        rhs_v[:, :, :].rearrange("p (i f) d -> p f i d", f=2)[:, f],
                                        ALU.add).then_inc(moved_v[f], 1)
                dve.wait_ge(o_ready, al(t, l, 1, 1))
                v.tensor_copy(o_t[:, :, :], bank(6)).then_inc(o_moved, 1)
                dve.wait_ge(att_ready, al(t, l, 1, 1))

            def routing(t):
                dve.wait_ge(scores_ready, t + 1)
                hold()
                for c in range(2):
                    for h in range(H):
                        did(v.max(best[:, c, h, :], ps[:, P * (H * c + h):P * (H * c + h + 1)]))
                settle(t, alone=True)
                for c in range(2):
                    for h in range(H):
                        did(v.max_index(besti[:, c, h, :], best[:, c, h, :], ps[:, P * (H * c + h):P * (H * c + h + 1)]))
                did(v.tensor_tensor(cand[:, :, :, :], best[:, 0, :, :].unsqueeze(3).broadcast_to([P, H, K, K]),
                                    best[:, 1, :, :].unsqueeze(2).broadcast_to([P, H, K, K]), ALU.add))
                settle(t)
                did(v.tensor_copy(bestf[:, :, :, :], besti[:, :, :, :]))
                for h in range(H):
                    did(v.max(top[:, h, :], cand[:, h, :, :]))
                settle(t)
                v.tensor_tensor(shifted[:, :, :], top[:, :, :], top[:, :, 0:1].broadcast_to([P, H, K]),
                                    ALU.subtract).then_inc(top_shifted, 1)
                for h in range(H):
                    did(v.max_index(topi[:, h, :], top[:, h, :], cand[:, h, :, :].rearrange("p a b -> p (a b)")))
                settle(t)
                flat = topi[:, :, :].rearrange("p h k -> p (h k)")
                did(v.tensor_scalar(pos[:, 0, :], flat, 3, None, ALU.logical_shift_right))
                did(v.tensor_scalar(pos[:, 1, :], flat, 7, None, ALU.bitwise_and))
                settle(t)
                did(v.tensor_copy(posf[:, :, :], pos[:, :, :]))
                settle(t)
                for c in range(2):
                    did(v.tensor_tensor(hot[:, :, :], posf[:, c, :].unsqueeze(2).broadcast_to([P, SLOTS, K]),
                                        iota8.unsqueeze(1).broadcast_to([P, SLOTS, K]), ALU.is_equal))
                    settle(t)
                    hot4 = hot[:, :, :].rearrange("p (h k) a -> p h k a", h=H)
                    did(v.tensor_tensor(hot4, hot4, bestf[:, c, :, :].unsqueeze(2).broadcast_to([P, H, K, K]), ALU.mult))
                    settle(t)
                    did(v.tensor_reduce(half_i[:, c, :], hot[:, :, :], AX.X, ALU.add))
                    settle(t)
                did(v.scalar_tensor_tensor(idx_next[:, :], half_i[:, 0, :], float(P), half_i[:, 1, :], ALU.mult, ALU.add))
                dve.wait_ge(top_exped, t + 1)
                did(v.tensor_reduce(w_sum[:, :], w_exp[:, :, :], AX.X, ALU.add))
                settle(t)
                did(v.reciprocal(w_rec[:, :], w_sum[:, :]))
                settle(t)
                did(v.scalar_tensor_tensor(w_next[:, :].rearrange("p (h k) -> p h k", h=H), w_exp[:, :, :], 0.5,
                                           w_rec[:, :].unsqueeze(2).broadcast_to([P, H, K]), ALU.mult, ALU.mult))
                settle(t)

            def combine(t, c):
                did(v.tensor_tensor(prod[:, :, :], rows_got[:, CS * c:CS * (c + 1), 0:P],
                                    q_now[:, :].unsqueeze(1).broadcast_to([P, CS, P]), ALU.mult), c_done)
                settle(t, c_done)
                did(v.tensor_reduce(xd[:, :], prod[:, :, :], AX.X, ALU.add), c_done)
                settle(t, c_done)
                did(v.tensor_tensor(g1[:, :], xd[:, :], xd[:, :], ALU.mult), c_done)
                settle(t, c_done)
                did(v.tensor_scalar(g2[:, :], g1[:, :], 0.044715, 1.0, ALU.mult, ALU.add), c_done)
                settle(t, c_done)
                v.tensor_tensor(g3[:, :], g2[:, :], xd[:, :], ALU.mult).then_inc(u_ready, 1)
                dve.wait_ge(th_ready, at(t, CHUNKS, c + 1))
                did(v.scalar_tensor_tensor(g4[:, :], th[:, :], 1.0, xd[:, :], ALU.add, ALU.mult), c_done)
                settle(t, c_done)
                v.tensor_tensor(val[:, :], g4[:, :], w_now[:, CS * c:CS * (c + 1)], ALU.mult).then_inc(val_ready, 1)

            def landed(t, c):
                dve.wait_ge(got[c], at(t, 16 * CS, 16 * CS))

            def finish(t, tile):
                dve.wait_ge(up_done, at(t, CHUNKS, CHUNKS))
                v.tensor_tensor(tile, bank(UP, 0, P), h_now[:, :], ALU.add).then_inc(out_ready, 1)

            def hand_over_indices(t):
                v.tensor_copy(idx_now[:, :], idx_next[:, :]).then_inc(idx_ready, 1)

            def hand_over_rest(t):
                did(v.tensor_copy(w_now[:, :], w_next[:, :]))
                did(v.tensor_copy(q_now[:, :], normed[:, :]))
                did(v.tensor_copy(h_now[:, :], h0[:, :]))
                settle(t)

            def attend(t, h_tile, chunk):
                did(v.tensor_tensor(h0[:, :], h_tile, bias_sb[:, :], ALU.add))
                settle(t)
                layer_norm(t, h0[:, :])
                dve.wait_ge(proj_ready, t + 1)
                did(v.tensor_tensor(xs[:, :], bank(5, 0, P), rows_sb[:, 0:P], ALU.add))
                settle(t)
                layer_norm(t, xs[:, :])
                layer_start(t, 0)
                chunk(0)
                layer_solve(t, 0)
                did(v.tensor_tensor(xs[:, :], xs[:, :], bank(5, 0, P), ALU.add))
                settle(t)
                layer_norm(t, xs[:, :])
                did(v.tensor_tensor(xs2[:, :], xs[:, :], rows_sb[:, P:2 * P], ALU.add))
                settle(t)
                chunk(1)
                dve.wait_ge(ff2_ready, t + 1)
                did(v.tensor_tensor(xs[:, :], xs2[:, :], bank(5, 0, P), ALU.add))
                settle(t)
                layer_norm(t, xs[:, :])
                layer_start(t, 1)
                did(v.tensor_tensor(xs2[:, :], xs[:, :], h0[:, :], ALU.add))
                settle(t)
                chunk(2)
                layer_solve(t, 1)
                did(v.tensor_tensor(h0[:, :], xs2[:, :], bank(5, 0, P), ALU.add))
                settle(t)
                layer_norm(t, h0[:, :])
                routing(t)

            attend(0, h_tok[:, 0, :], lambda c: None)
            hand_over_indices(0)
            hand_over_rest(0)
            a_tile[v_done] = count[v_done]
            a_tile[c_done] = 5 * CHUNKS
            with dve.Fori(1, TILES) as t:
                count[v_done] = count[c_done] = 0

                def chunk(c):
                    landed(t - 1, c)
                    combine(t - 1, c)

                attend(t, h_tok[:, bass.ds(t, 1), :].rearrange("p t q -> p (t q)"), chunk)
                landed(t - 1, CHUNKS - 1)
                hand_over_indices(t)
                combine(t - 1, CHUNKS - 1)
                finish(t - 1, h_tok[:, bass.ds(t - 1, 1), :].rearrange("p t q -> p (t q)"))
                dve.wait_ge(out_ready, t)
                hand_over_rest(t)
            assert count[v_done] == a_tile[v_done] and count[c_done] == a_tile[c_done]
            count[c_done] = 0
            for c in range(CHUNKS):
                landed(TILES - 1, c)
                combine(TILES - 1, c)
            finish(TILES - 1, h_tok[:, TILES - 1, :])

        @block.tensor
        def _(pe):
            pe.wait_ge(x_landed, 16)
            for n in range(2 * WG):
                grp, half = n // 2, n % 2
                pe.wait_ge(masked, n + 1)
                w = ring[0:GP, n % RING, :].rearrange("p (e c q) -> p e c q", e=S // 2, c=CG)
                for k in range(CG):
                    c = CG * grp + k
                    for j in range(2):
                        last = nc.tensor.matmul(
                            bank(half)[B * j:B * (j + 1), :].rearrange("p (e q) -> p e q", e=S // 4),
                            x_sb[:, B * c:B * (c + 1)], w[:, S // 4 * j:S // 4 * (j + 1), k, :],
                            start=(c == 0), stop=(c == GC - 1))
                last.then_inc(w_used, 1)
                if grp == WG - 1:
                    pe.nop(nofuse=True)
                    nc.tensor.drain().then_inc(h_summed, 1)

            pe.wait_ge(mats_landed, 16)
            pe.wait_ge(consts_landed, 16 * (3 + P // S))
            mm = nc.tensor.matmul

            def turn_norm(t, n):
                pe.wait_ge(norm_ready, at(t, NORMS, n + 1))
                nc.tensor.transpose(bank(6, 0, P), normed[:, :], ident).then_inc(norm_turned, 1)

            def norm_t_ready(t, n):
                pe.wait_ge(norm_moved, at(t, NORMS, n + 1))

            def layer_start(t, l):
                w = f"slow{l}"
                norm_t_ready(t, 1 + 2 * l)
                for n in range(2):
                    last = mm(bank(n), normed_t[:, :], mat(w, n, H * D), start=True, stop=True)
                last.then_inc(qk_ready, 1)
                mm(bank(2), normed_t[:, :], mat(w, 2, H * D), start=True, stop=True)
                mm(bank(3, 0, H), normed_t[:, :], mats[:, OFF[w] + 3 * H * D:OFF[w] + QKV],
                   start=True, stop=True).then_inc(v_ready, 1)
                pairs = eqk[:, :, :].rearrange("p (i f) d -> p i (f d)", f=2)
                pe.wait_ge(e_ready, al(t, l, 2 * H, H))
                for i in range(HP):
                    last = nc.tensor.transpose(bank(1, P * i, P * (i + 1)), pairs[:, HP + i, :], ident)
                last.then_inc(ek_turned, 1)
                pe.wait_ge(tb_ready, al(t, l, 1, 1))
                pe.wait_ge(ekc_ready, al(t, l, 1, 1))
                for i in range(HP):
                    last = nc.tensor.transpose(bank(3, P * i, P * (i + 1)),
                                               ekc[:, :, :].rearrange("p (i f) d -> p i (f d)", f=2)[:, i, :], ident)
                last.then_inc(ekc_turned, 1)
                pe.wait_ge(eq_ready, al(t, l, 1, 1))
                for i in range(HP):
                    last = nc.tensor.transpose(bank(0, P * i, P * (i + 1)), pairs[:, i, :], ident)
                last.then_inc(eq_turned, 1)

            def layer_solve(t, l):
                def col(f, n, i, w=P):
                    return bank(SOLVE[f][n], w * i, w * (i + 1))

                def scores(n, lhs, rhs):
                    for i in range(HP):
                        for f in range(2):
                            last = mm(col(f, n, i), lhs[D * f:D * (f + 1), i, :], rhs[D * f:D * (f + 1), i, :],
                                      start=True, stop=True)
                            if i == HP - 1:
                                last.then_inc(product[f], 1)

                def multiply(f, n, lhs, rhs, w=P):
                    for i in range(HP):
                        last = mm(col(f, n, i, w), lhs[:, i, :], rhs[:, i, :], start=True, stop=True)
                    last.then_inc(product[f], 1)

                def by_vector(f, n):
                    pe.wait_ge(moved_v[f], al(t, l, MOVED_V, n))

                def by_scalar(f, n):
                    pe.wait_ge(moved_c[f], al(t, l, MOVED_C, n))

                pe.wait_ge(ek_moved, al(t, l, 1, 1))
                pe.wait_ge(ekc_moved, al(t, l, 1, 1))
                pe.wait_ge(eq_moved, al(t, l, 1, 1))
                scores(0, ek_t, ekc_t)
                scores(1, ekc_t, ek_t)
                scores(2, ek_t, eq_t)
                for f in range(2):
                    by_scalar(f, C_U)
                    by_vector(f, V_T2)
                    multiply(f, 1, u_raw[f], t2[f])
                for f in range(2):
                    by_vector(f, V_A2)
                    multiply(f, 0, t2t[f], a2[f])
                    multiply(f, 1, a2[f], t2t[f])
                for f in range(2):
                    by_scalar(f, C_T4T)
                    multiply(f, 0, u_raw[f], t4[f])
                for f in range(2):
                    by_vector(f, V_A4)
                    multiply(f, 1, a4[f], t4t[f])
                pe.wait_ge(rhs_ready, al(t, l, 1, 1))
                rhs = rhs_v[:, :, :].rearrange("p (i f) d -> p f i d", f=2)
                for f in range(2):
                    by_scalar(f, C_T8T)
                    multiply(f, 0, t8t[f], rhs[:, f], D)
                for f in range(2):
                    by_scalar(f, C_Y)
                    multiply(f, 1, u8[f], y[f], D)
                for f in range(2):
                    by_vector(f, V_R)
                    multiply(f, 0, t8t[f], r2[f], D)
                for f in range(2):
                    by_scalar(f, C_Z)
                    pe.nop(nofuse=True)
                    for i in range(HP):
                        last = mm(bank(6)[D * f:D * (f + 1), P * i:P * (i + 1)], z[f][:, i, :], s_m[f][:, i, :],
                                  start=True, stop=True)
                last.then_inc(o_ready, 1)
                pe.wait_ge(o_moved, al(t, l, 1, 1))
                for i in range(HP):
                    last = mm(bank(5, 0, P), o_t[:, i, :], mat(f"out{l}", i), start=(i == 0), stop=(i == HP - 1))
                last.then_inc(att_ready, 1)

            def feed_forward(t):
                norm_t_ready(t, 2)
                for n in range(FC):
                    last = mm(bank(0, P * n, P * (n + 1)), mat("w1", n), normed_t[:, :], start=True, stop=True)
                last.then_inc(ff1_ready, 1)
                for n in range(FC):
                    pe.wait_ge(ff1_moved, at(t, FC, n + 1))
                    last = mm(bank(5, 0, P), ff[:, n, :], mat("w2", n), start=(n == 0), stop=(n == FC - 1))
                last.then_inc(ff2_ready, 1)

            def routing(t):
                norm_t_ready(t, 4)
                for h in range(H):
                    last = mm(ps[:, 4 * 512 + P * h:4 * 512 + P * (h + 1)], mat("wq", h), normed_t[:, :],
                              start=True, stop=True)
                last.then_inc(qh_ready, 1)
                pe.wait_ge(qh_moved, at(t, H, H))
                for h in range(H):
                    for c in range(2):
                        last = mm(ps[:, P * (H * c + h):P * (H * c + h + 1)], qh_t[D * c:D * (c + 1), h, :],
                                  mat("keys", h)[D * c:D * (c + 1), :], start=True, stop=True)
                last.then_inc(scores_ready, 1)

            def combine(t, c):
                pe.wait_ge(diag_ready, at(t, CHUNKS, c + 1))
                for k in range(CS):
                    s = CS * c + k
                    last = mm(bank(UP, 0, P), diag[:, k, :], rows_got[:, s, P:2 * P],
                              start=(s == 0), stop=(s == SLOTS - 1))
                last.then_inc(up_done, 1)

            def attend(t, chunk):
                turn_norm(t, 0)
                norm_t_ready(t, 0)
                mm(bank(5, 0, P), normed_t[:, :], mat("ip", 0), start=True, stop=True).then_inc(proj_ready, 1)
                turn_norm(t, 1)
                layer_start(t, 0)
                chunk(0)
                layer_solve(t, 0)
                chunk(1)
                turn_norm(t, 2)
                feed_forward(t)
                turn_norm(t, 3)
                layer_start(t, 1)
                chunk(2)
                layer_solve(t, 1)
                turn_norm(t, 4)
                routing(t)
                chunk(3)

            attend(0, lambda c: None)
            with pe.Fori(1, TILES) as t:
                attend(t, lambda c: combine(t - 1, c))
            for c in range(CHUNKS):
                combine(TILES - 1, c)


def constants():
    i = np.arange(P)
    row, col = i[:, None], i[None, :]
    same = row // S == col // S

    def off_diagonal(n):
        return (row // (2 * n) == col // (2 * n)) & (row // n % 2 == 1) & (col // n % 2 == 0)

    f = np.concatenate([np.eye(P), off_diagonal(8).T, same & (row <= col), np.tile(np.arange(K), (P, 1))], axis=1)
    m = np.concatenate([off_diagonal(1), off_diagonal(1).T, off_diagonal(2), off_diagonal(4)], axis=1)
    return f.astype(np.float32), m.astype(np.int32)


def kernel(x, L0_tok_weight, L0_tok_bias, L0_tok_mask, L0_attn_ip_w, L0_attn_ip_b, L0_attn_fw_ln_g, L0_attn_fw_ln_b,
           L0_attn_fw_slow_w, L0_attn_fw_out_w, L0_attn_ff_ln_g, L0_attn_ff_ln_b, L0_attn_ff_w1, L0_attn_ff_b1,
           L0_attn_ff_w2, L0_attn_ff_b2, L0_ffn_Wq, L0_ffn_bq, L0_ffn_keys, L0_ffn_w_down_embed, L0_ffn_w_up_embed):
    import concourse.bacc as bacc
    from concourse.bass_utils import run_bass_kernel_spmd

    def slow(w):
        w = np.asarray(w).reshape(H, 3 * D + 1, P)
        parts = [w[:, D * n:D * (n + 1)].reshape(H * D, P) for n in range(3)] + [w[:, 3 * D]]
        return np.concatenate(parts, axis=0).T

    def chunked(w):
        w = np.asarray(w)
        return w.reshape(w.shape[0], -1, P).transpose(2, 1, 0).reshape(P, -1)

    def column(v):
        return np.asarray(v).reshape(-1, P).T

    packed = np.concatenate([
        np.asarray(L0_attn_ip_w).T, slow(L0_attn_fw_slow_w[0]), slow(L0_attn_fw_slow_w[1]),
        chunked(L0_attn_fw_out_w[0]), chunked(L0_attn_fw_out_w[1]),
        np.asarray(L0_attn_ff_w1).T, chunked(L0_attn_ff_w2), np.asarray(L0_ffn_Wq).T,
        np.asarray(L0_ffn_keys).transpose(1, 3, 0, 2).reshape(P, H * P),
        column(L0_attn_fw_ln_g[0]), column(L0_attn_fw_ln_b[0]), column(L0_attn_fw_ln_g[1]), column(L0_attn_fw_ln_b[1]),
        column(L0_attn_ff_ln_g), column(L0_attn_ff_ln_b), column(L0_attn_ff_b1), column(L0_ffn_bq)], axis=1)
    assert packed.shape == (P, PACKED)
    fconst, iconst = constants()
    arrays = {
        "weight": np.asarray(L0_tok_weight),
        "x_t": np.asarray(x).T.reshape(GP, GC * B),
        "mask": np.asarray(L0_tok_mask),
        "packed": packed,
        "bias": np.asarray(L0_tok_bias),
        "rows": np.concatenate([np.asarray(L0_attn_ip_b), np.asarray(L0_attn_ff_b2)]),
        "fconst": fconst,
        "iconst": iconst,
        "table": np.concatenate([np.asarray(L0_ffn_w_down_embed), np.asarray(L0_ffn_w_up_embed)], axis=1),
    }
    nc = bacc.Bacc("TRN2", target_bir_lowering=False, num_devices=1)
    arrays = {k: np.ascontiguousarray(a) for k, a in arrays.items()}
    args = [nc.dram_tensor(k, a.shape, mybir.dt.from_np(a.dtype), kind="ExternalInput").ap() for k, a in arrays.items()]
    h_dram = nc.dram_tensor("h_dram", (B, S, P), F32, kind="Internal").ap()
    out = nc.dram_tensor("out", (B, S, P), F32, kind="ExternalOutput").ap()
    build(nc, *args, h_dram, out)
    r = run_bass_kernel_spmd(nc, [arrays], core_ids=[0])
    return r.results[0]["out"]
```

```python
from contextlib import ExitStack

import numpy as np
import concourse.bass as bass
from concourse import mybir

F32 = mybir.dt.float32
U32 = mybir.dt.uint32
I32 = mybir.dt.int32
ALU = mybir.AluOpType
ACT = mybir.ActivationFunctionType
AX = mybir.AxisListType

B, G = 64, 5000
S, P = 16, 128
H, D = 8, 64
HP = H // 2
FC = 4
K = 8
SLOTS = H * K
TILES = B * S // P
GP = 125
GC = G // GP
CG = 4
WG = GC // CG
RING = 4
EPS = 1e-5

QKV = 3 * H * D + H
OFF = {}
_at = 0
for _name, _n in (("ip", P), ("slow0", QKV), ("slow1", QKV), ("out0", HP * P), ("out1", HP * P),
                  ("w1", FC * P), ("w2", FC * P), ("wq", H * P), ("keys", H * P),
                  ("g0", 1), ("b0", 1), ("g1", 1), ("b1", 1), ("gf", 1), ("bf", 1), ("fb1", FC), ("bq", H)):
    OFF[_name] = _at
    _at += _n
PACKED = _at

(P_U, P_S, P_T2, P_A2, P_T4, P_T4T, P_A4, P_T8T, P_Y, P_W, P_Z) = range(1, 12)
PRODUCTS = 11
(V_T2T, V_U8, V_S, V_A2, V_A4, V_R) = range(1, 7)
MOVED_V = 6
(C_U, C_T2, C_T4, C_T4T, C_T8T, C_Y, C_Z) = range(1, 8)
MOVED_C = 7
NORMS = 5
CHUNKS = 4
CS = SLOTS // CHUNKS
PARTS = 8
SP = SLOTS // PARTS


def build(nc, weight, x_t, mask, packed, bias, rows, fconst, iconst, table, h_dram, out):
    with ExitStack() as ctx:
        def sb(name, shape, dt=F32):
            return ctx.enter_context(nc.sbuf_tensor(name, shape, dt))

        def sem(name):
            return ctx.enter_context(nc.semaphore(name))

        mats = sb("mats", [P, PACKED])
        bias_sb = sb("bias_sb", [P, P])
        rows_sb = sb("rows_sb", [P, 2 * P])
        fc_sb = sb("fc_sb", [P, 3 * P + K])
        ic_sb = sb("ic_sb", [P, 3 * P], I32)
        mask_mem = sb("mask_mem", [P, GC * P])
        x_mem = sb("x_mem", [P, GC * B])
        mask_sb, x_sb = mask_mem[0:GP, :], x_mem[0:GP, :]
        ring = sb("ring", [P, RING, S // 2 * CG * P])
        rows_got = ring[:, :, :].rearrange("p r (s n) -> p (r s) n", n=2 * P)
        h_cols = sb("h_cols", [P, 2, 512])
        h_tok = sb("h_tok", [P, TILES, P])
        ident = fc_sb[:, 0:P]
        mask_u8 = fc_sb[:, P:2 * P]
        mask_s = fc_sb[:, 2 * P:3 * P]
        iota8 = fc_sb[:, 3 * P:3 * P + K]
        m1t, m2, m4 = (ic_sb[:, P * n:P * (n + 1)] for n in range(3))

        def mat(name, n, w=P):
            return mats[:, OFF[name] + n * w:OFF[name] + (n + 1) * w]

        stats = sb("stats", [P, 6])
        mv = sb("mv", [P, 2])
        var = sb("var", [P, 1])
        rs = sb("rs", [P, 1])
        rs2 = sb("rs2", [P, 1])
        var2 = sb("var2", [P, 1])
        normed_f, normed_s = sb("normed_f", [P, P]), sb("normed_s", [P, P])
        normed_ft, normed_st = sb("normed_ft", [P, P]), sb("normed_st", [P, P])
        normed = [normed_f, normed_f, normed_f, normed_s, normed_s]
        normed_t = [normed_ft, normed_ft, normed_ft, normed_st, normed_st]
        h_f = sb("h_f", [P, P])
        xs = sb("xs", [P, P])
        xs_b = sb("xs_b", [P, P])
        res = sb("res", [P, P])
        h_s = sb("h_s", [P, P])
        ff = x_mem[:, (H + HP) * P:(H + HP + FC) * P].rearrange("p (n q) -> p n q", n=FC)
        nmax = sb("nmax", [P, 2 * H])
        esum = sb("esum", [P, 2 * H])
        rsum = sb("rsum", [P, 2 * H])
        tb = sb("tb", [P, H])
        beta = sb("beta", [P, H])
        rb = sb("rb", [P, H])
        rrb = sb("rrb", [P, H])
        eqk = sb("eqk", [P, 2 * H, D])
        ekc = sb("ekc", [P, H, D])
        rhs_v = [sb(f"rhs_v{n}", [P, H, D]) for n in range(2)]
        ek_t = h_cols[:, 0, :].rearrange("p (i q) -> p i q", i=HP)
        ekc_t = sb("ekc_t", [P, HP, 2, P])
        eq_t = sb("eq_t", [P, HP, 2, P])

        def halves(name, width=P):
            return [sb(f"{name}{g}", [P, H // 2, width]) for g in range(2)]

        u_raw, u8, s_m = halves("u_raw"), halves("u8"), halves("s_m")
        t2, t2t, a2, a4 = halves("t2_"), halves("t2t_"), halves("a2_"), halves("a4_")
        t4, t4t, t8t = halves("t4_"), halves("t4t_"), halves("t8t_")
        y = halves("y", D)
        z = y
        o_t = x_mem[:, H * P:H * P + HP * P].rearrange("p (i q) -> p i q", i=HP)
        qh_t = x_mem[:, 0:H * P].rearrange("p (h q) -> p h q", h=H)
        best = sb("best", [P, 2, H, K])
        besti = sb("besti", [P, 2, H, K], U32)
        bestf = sb("bestf", [P, 2, H, K])
        top = sb("top", [P, H, K])
        topi = sb("topi", [P, H, K], U32)
        pos = sb("pos", [P, 2, SLOTS], U32)
        posf = sb("posf", [P, 2, SLOTS])
        half_i = sb("half_i", [P, 2, SLOTS])
        shifted = sb("shifted", [P, H, K])
        w_exp = sb("w_exp", [P, H, K])
        w_sum = sb("w_sum", [P, H])
        w_rec = sb("w_rec", [P, H])
        w_next = sb("w_next", [P, SLOTS])
        idx_next = sb("idx_next", [P, SLOTS], U32)
        w_now = sb("w_now", [P, SLOTS])
        idx_now = sb("idx_now", [P, SLOTS], U32)
        q_now = sb("q_now", [P, P])
        h_now = sb("h_now", [P, P])
        prod = mask_mem[:, 0:SP * P].rearrange("p (s q) -> p s q", s=SP)
        xd = sb("xd", [P, CS])
        g1, g2 = sb("g1_", [P, CS]), sb("g2_", [P, CS])
        g3, g4 = sb("g3_", [P, CS]), sb("g4_", [P, CS])
        th = sb("th", [P, CS])
        val = sb("val", [P, SLOTS])
        diag = mask_mem[:, CS * P:2 * CS * P].rearrange("p (b s q) -> p b s q", b=2, s=SP)
        cand = mask_mem[:, 2 * CS * P:2 * CS * P + H * K * K].rearrange("p (h a b) -> p h a b", h=H, a=K)
        hot = mask_mem[:, 2 * CS * P + H * K * K:2 * CS * P + 2 * H * K * K].rearrange("p (s a) -> p s a", a=K)

        ps = ctx.enter_context(nc.psum_tensor("ps", [P, 8 * 512], F32))

        def bank(n, lo=0, hi=512):
            return ps[:, 512 * n + lo:512 * n + hi]

        QB, KB, VB = 1, 0, 2
        SOLVE = ((3, 4), (5, 6))
        UP = 7
        NORM_BANK = (3, 2, 3, 2, 3)
        SCORE_BANK = (2, 0, 1, 2)

        w_landed = [sem(f"w_landed{n}") for n in range(RING)]
        x_landed, mask_landed, mats_landed = sem("x_landed"), sem("mask_landed"), sem("mats_landed")
        consts_landed = sem("consts_landed")
        masked, w_used, h_summed, h_copied = sem("masked"), sem("w_used"), sem("h_summed"), sem("h_copied")
        h_stored, h_loaded = sem("h_stored"), sem("h_loaded")
        f_done, s_done, c_done = sem("f_done"), sem("s_done"), sem("c_done")
        setup_done = sem("setup_done")
        norm_ready = [sem(f"norm_ready{n}") for n in range(NORMS)]
        norm_turned = [sem(f"norm_turned{n}") for n in range(NORMS)]
        norm_moved = [sem(f"norm_moved{n}") for n in range(NORMS)]
        proj_ready, proj_used = sem("proj_ready"), sem("proj_used")
        qk_ready, v_ready, nmax_ready = sem("qk_ready"), sem("v_ready"), sem("nmax_ready")
        tb_ready, e_ready, eq_ready, ekc_ready = sem("tb_ready"), sem("e_ready"), sem("eq_ready"), sem("ekc_ready")
        ek_turned, eq_turned, ekc_turned = sem("ek_turned"), sem("eq_turned"), sem("ekc_turned")
        ek_moved, eq_moved, ekc_moved = sem("ek_moved"), sem("eq_moved"), sem("ekc_moved")
        product = [sem(f"product{f}") for f in range(2)]
        moved_v = [sem(f"moved_v{f}") for f in range(2)]
        moved_c = [sem(f"moved_c{f}") for f in range(2)]
        rhs_ready, beta_ready = sem("rhs_ready"), sem("beta_ready")
        o_ready, o_moved, att_ready = sem("o_ready"), sem("o_moved"), sem("att_ready")
        scores_used = sem("scores_used")
        ff1_ready, ff1_moved, ff2_ready = sem("ff1_ready"), sem("ff1_moved"), sem("ff2_ready")
        qh_ready, qh_moved, scores_ready = sem("qh_ready"), sem("qh_moved"), sem("scores_ready")
        top_shifted, top_exped, idx_ready = sem("top_shifted"), sem("top_exped"), sem("idx_ready")
        got = [sem(f"got{n}") for n in range(CHUNKS)]
        u_ready, th_ready, val_ready, diag_ready, up_done = (sem("u_ready"), sem("th_ready"), sem("val_ready"),
                                                             sem("diag_ready"), sem("up_done"))
        out_ready, out_stored = sem("out_ready"), sem("out_stored")

        def at(t, a_tile, n):
            return t * a_tile + n

        def al(t, l, a_layer, n):
            return t * (2 * a_layer) + (l * a_layer + n)

        block = ctx.enter_context(nc.Block())

        @block.sync
        def _(sp):
            sp.dma_start(x_sb[:, :], x_t).then_inc(x_landed, 16)
            w_view = weight.rearrange("e (p c) q -> p e (c q)", p=GP)
            for n in range(2 * WG):
                grp, half = n // 2, n % 2
                if n >= RING:
                    sp.wait_ge(w_used, n - RING + 1)
                sp.dma_start(ring[0:GP, n % RING, :].rearrange("p (e k) -> p e k", e=S // 2),
                             w_view[:, S // 2 * half:S // 2 * (half + 1), CG * P * grp:CG * P * (grp + 1)]
                             ).then_inc(w_landed[n % RING], 16)
            h_view = h_dram.rearrange("b (f j i) q -> j b f (i q)", f=2, j=2)
            sp.wait_ge(h_copied, 2)
            for j in range(2):
                sp.dma_start(h_view[j], h_cols[B * j:B * (j + 1), :, :]).then_inc(h_stored, 16)
            sp.wait_ge(h_stored, 32)
            sp.dma_start(h_tok[:, :, :], h_dram.rearrange("(t a) e q -> (a e) t q", t=TILES)).then_inc(h_loaded, 16)
            out_view = out.rearrange("(t a) e q -> t (a e) q", t=TILES)
            with sp.Fori(0, TILES) as t:
                sp.wait_ge(out_ready, t + 1)
                sp.dma_start(out_view[bass.ds(t, 1), :, :].rearrange("t p q -> p (t q)"),
                             h_tok[:, bass.ds(t, 1), :].rearrange("p t q -> p (t q)")).then_inc(out_stored, 16)
            sp.wait_ge(out_stored, 16 * TILES)

        @block.gpsimd
        def _(pool):
            def gather(t, first):
                pool.wait_ge(idx_ready, t + 1)
                for c in range(CHUNKS):
                    if not first:
                        pool.wait_ge(up_done, at(t, PARTS, 2 * (c + 1) - PARTS))
                    pool.nop(nofuse=True)
                    for s in range(CS * c, CS * (c + 1)):
                        pool.indirect_dma_start(
                            out=rows_got[:, s, :], out_offset=None, in_=table,
                            in_offset=bass.IndirectOffsetOnAxis(ap=idx_now[:, s:s + 1], axis=0)
                        ).then_inc(got[c], 16)

            gather(0, True)
            with pool.Fori(1, TILES) as t:
                gather(t, False)

        @block.scalar
        def _(act):
            act.dma_start(mask_sb, mask.rearrange("(p c) q -> p (c q)", p=GP)).then_inc(mask_landed, 16)
            act.dma_start(fc_sb[:, :], fconst).then_inc(consts_landed, 16)
            act.dma_start(ic_sb[:, :], iconst).then_inc(consts_landed, 16)
            for n in range(P // S):
                act.dma_start(bias_sb[S * n:S * (n + 1), :], bias).then_inc(consts_landed, 16)
            act.dma_start(rows_sb[:, :], rows.partition_broadcast(P)).then_inc(consts_landed, 16)
            act.dma_start(mats[:, :], packed).then_inc(mats_landed, 16)
            act.wait_ge(consts_landed, 16 * (3 + P // S))
            act.wait_ge(mats_landed, 16)
            for f in range(2):
                act.wait_ge(h_summed, f + 1)
                nc.scalar.activation(h_cols[:, f, :], bank(f), ACT.Copy).then_inc(h_copied, 1)

            AFFINE = (None, ("g0", "b0"), ("gf", "bf"), ("g1", "b1"), None)

            def move_norm(t, n):
                act.wait_ge(norm_turned[n], t + 1)
                src = bank(NORM_BANK[n], 0, P)
                if AFFINE[n] is None:
                    nc.scalar.activation(normed_t[n][:, :], src, ACT.Copy).then_inc(norm_moved[n], 1)
                else:
                    g, b = AFFINE[n]
                    nc.scalar.activation(normed_t[n][:, :], src, ACT.Identity,
                                         bias=mat(b, 0, 1), scale=mat(g, 0, 1)).then_inc(norm_moved[n], 1)

            def beta(t, l):
                act.wait_ge(beta_ready, al(t, l, 1, 1))
                nc.scalar.activation(tb[:, :], bank(QB, 0, H), ACT.Tanh, scale=0.5).then_inc(tb_ready, 1)

            def exps(t, l, n):
                act.wait_ge(nmax_ready, al(t, l, 2, n + 1))
                for h in range(H):
                    j = (1 - n) * H + h
                    nc.scalar.activation(eqk[:, j, :], bank((KB, QB)[n], D * h, D * (h + 1)), ACT.Exp,
                                         bias=nmax[:, j:j + 1], accum_out=esum[:, j:j + 1]).then_inc(e_ready, 1)

            def move_keys(t, l):
                act.wait_ge(ek_turned, al(t, l, 1, 1))
                nc.scalar.activation(ek_t, bank(KB), ACT.Copy).then_inc(ek_moved, 1)

            def move_rest(t, l):
                def spread(dst, n, s):
                    for f in range(2):
                        rows = slice(D * f, D * (f + 1))
                        nc.scalar.activation(dst[rows, :, f, :], bank(n)[rows, :].rearrange("p (i q) -> p i q", i=HP),
                                             ACT.Copy).then_inc(s, 1)

                act.wait_ge(ekc_turned, al(t, l, 1, 1))
                spread(ekc_t, VB, ekc_moved)
                act.wait_ge(eq_turned, al(t, l, 1, 1))
                spread(eq_t, QB, eq_moved)

            def move(t, l, p, dst, n, width=P):
                for f in range(2):
                    act.wait_ge(product[f], al(t, l, PRODUCTS, p))
                    nc.scalar.activation(dst[f][:, :, :], bank(SOLVE[f][n], 0, H // 2 * width),
                                         ACT.Copy).then_inc(moved_c[f], 1)

            def move_out(t, l):
                act.wait_ge(o_ready, al(t, l, 1, 1))
                nc.scalar.activation(o_t[:, :, :], bank(3), ACT.Copy).then_inc(o_moved, 1)

            def relu(t):
                act.wait_ge(ff1_ready, t + 1)
                for n in range(FC):
                    nc.scalar.activation(ff[:, n, :], bank(4, P * n, P * (n + 1)), ACT.Relu,
                                         bias=mat("fb1", n, 1)).then_inc(ff1_moved, 1)

            def product_queries(t):
                act.wait_ge(qh_ready, t + 1)
                for h in range(H):
                    nc.scalar.activation(qh_t[:, h, :], ps[:, P * h:P * (h + 1)], ACT.Identity,
                                         bias=mat("bq", h, 1)).then_inc(qh_moved, 1)

            def top_exp(t):
                act.wait_ge(top_shifted, t + 1)
                nc.scalar.activation(w_exp[:, :, :], shifted[:, :, :], ACT.Exp).then_inc(top_exped, 1)

            def gelu(t, c):
                act.wait_ge(u_ready, at(t, CHUNKS, c + 1))
                nc.scalar.activation(th[:, :], g3[:, :], ACT.Tanh, scale=0.7978845608028654).then_inc(th_ready, 1)

            def diagonals(t, m):
                act.wait_ge(val_ready, at(t, CHUNKS, m * SP // CS + 1))
                if m >= 2:
                    act.wait_ge(up_done, at(t, PARTS, m - 1))
                for k in range(SP):
                    s = SP * m + k
                    last = nc.scalar.activation(diag[:, m % 2, k, :], ident, ACT.Copy, scale=val[:, s:s + 1])
                last.then_inc(diag_ready, 1)

            def first_alone(u):
                move_norm(u, 0)
                move_norm(u, 1)
                beta(u, 0)
                exps(u, 0, 0)
                exps(u, 0, 1)
                move_keys(u, 0)
                move_rest(u, 0)
                move(u, 0, P_U, u_raw, 0)
                move(u, 0, P_T2, t2, 0)
                move(u, 0, P_T4, t4, 1)
                move(u, 0, P_T4T, t4t, 0)
                move(u, 0, P_T8T, t8t, 0)
                move(u, 0, P_Y, y, 1, D)
                move(u, 0, P_Z, z, 1, D)
                move_out(u, 0)
                move_norm(u, 2)
                relu(u)

            def step(t, u, c, d):
                if d is not None:
                    diagonals(d, 6)
                    diagonals(d, 7)
                move_norm(t, 3)
                beta(t, 1)
                exps(t, 1, 0)
                exps(t, 1, 1)
                move_keys(t, 1)
                if u is not None:
                    move_norm(u, 0)
                move_rest(t, 1)
                if c is not None:
                    gelu(c, 0)
                move(t, 1, P_U, u_raw, 0)
                move(t, 1, P_T2, t2, 0)
                if c is not None:
                    diagonals(c, 0)
                move(t, 1, P_T4, t4, 1)
                move(t, 1, P_T4T, t4t, 0)
                if u is not None:
                    move_norm(u, 1)
                    beta(u, 0)
                if c is not None:
                    diagonals(c, 1)
                move(t, 1, P_T8T, t8t, 0)
                move(t, 1, P_Y, y, 1, D)
                if u is not None:
                    exps(u, 0, 0)
                move(t, 1, P_Z, z, 1, D)
                if u is not None:
                    exps(u, 0, 1)
                move_out(t, 1)
                if u is not None:
                    move_keys(u, 0)
                    move_rest(u, 0)
                if c is not None:
                    gelu(c, 1)
                move_norm(t, 4)
                if c is not None:
                    diagonals(c, 2)
                if u is not None:
                    move(u, 0, P_U, u_raw, 0)
                    move(u, 0, P_T2, t2, 0)
                product_queries(t)
                if c is not None:
                    diagonals(c, 3)
                if u is not None:
                    move(u, 0, P_T4, t4, 1)
                    move(u, 0, P_T4T, t4t, 0)
                    move(u, 0, P_T8T, t8t, 0)
                    move(u, 0, P_Y, y, 1, D)
                top_exp(t)
                if c is not None:
                    gelu(c, 2)
                if u is not None:
                    move(u, 0, P_Z, z, 1, D)
                    move_out(u, 0)
                if c is not None:
                    diagonals(c, 4)
                if u is not None:
                    move_norm(u, 2)
                    relu(u)
                if c is not None:
                    diagonals(c, 5)
                    gelu(c, 3)

            first_alone(0)
            step(0, 1, None, None)
            step(1, 2, 0, None)
            with act.Fori(2, TILES - 1) as t:
                step(t, t + 1, t - 1, t - 2)
            step(TILES - 1, None, TILES - 2, TILES - 3)
            diagonals(TILES - 2, 6)
            diagonals(TILES - 2, 7)
            for c in range(CHUNKS):
                gelu(TILES - 1, c)
                for m in range(2 * c, 2 * c + 2):
                    diagonals(TILES - 1, m)

        @block.vector
        def _(dve):
            v = nc.vector

            class Line:

                def __init__(self, done, a_tile=None):
                    self.done, self.a_tile, self.t, self.n = done, a_tile, 0, 0

                def start(self, t):
                    if isinstance(self.t, int) and self.a_tile is None and self.n:
                        self.a_tile = self.n
                    assert self.n in (0, self.a_tile)
                    self.t, self.n = t, 0

                def did(self, instruction):
                    self.n += 1
                    return instruction.then_inc(self.done, 1)

                def settle(self, alone=False):
                    dve.wait_ge(self.done, at(self.t, self.a_tile, self.n) if self.a_tile else self.n)
                    if alone:
                        dve.nop(nofuse=True)

            first, second = Line(f_done), Line(s_done)
            experts = Line(c_done, 1 + 2 * PARTS + 3 * CHUNKS)

            def hold():
                dve.nop(nofuse=True)

            dve.wait_ge(consts_landed, 16 * (3 + P // S))
            for dst in (ekc_t, eq_t):
                v.memset(dst[:, :, :, :], 0.0).then_inc(setup_done, 1)
            for dst in (*t2t, *a2, *a4):
                v.tensor_copy(dst[:, :, :], ident.unsqueeze(1).broadcast_to([P, HP, P])).then_inc(setup_done, 1)

            dve.wait_ge(mask_landed, 16)
            for n in range(2 * WG):
                grp = n // 2
                w = ring[0:GP, n % RING, :].rearrange("p (e k) -> p e k", e=S // 2)
                m = mask_sb[:, CG * P * grp:CG * P * (grp + 1)]
                dve.wait_ge(w_landed[n % RING], 16 * (n // RING + 1))
                v.tensor_tensor(w, w, m.unsqueeze(1).broadcast_to([GP, S // 2, CG * P]), ALU.mult).then_inc(masked, 1)
            dve.wait_ge(setup_done, 8)
            dve.wait_ge(h_loaded, 16)
            dve.wait_ge(mats_landed, 16)

            def layer_norm(line, n, src):
                line.did(v.bn_stats(stats[:, :], src))
                line.settle(alone=True)
                line.did(v.bn_aggr(mv[:, :], stats[:, :]))
                line.settle()
                line.did(v.tensor_scalar(var[:, :], mv[:, 1:2], EPS, None, ALU.add))
                line.settle()
                line.did(v.tensor_scalar(rs[:, :].bitcast(I32), var[:, :].bitcast(I32), -0.5, float(0x5F3759DF),
                                         ALU.mult, ALU.add))
                line.did(v.tensor_scalar(var2[:, :], var[:, :], -0.5, None, ALU.mult))
                line.settle()
                for _ in range(3):
                    line.did(v.scalar_tensor_tensor(rs2[:, :], rs[:, :], var2[:, :], rs[:, :], ALU.mult, ALU.mult))
                    line.settle()
                    line.did(v.scalar_tensor_tensor(rs[:, :], rs2[:, :], 1.5, rs[:, :], ALU.add, ALU.mult))
                    line.settle()
                v.tensor_scalar(normed[n][:, :], src, mv[:, 0:1], rs[:, :], ALU.subtract,
                                ALU.mult).then_inc(norm_ready[n], 1)

            def maxima(t, l, n):
                j = (1 - n) * H
                dve.wait_ge(qk_ready, al(t, l, 2, n + 1))
                v.tensor_reduce(nmax[:, j:j + H], bank((KB, QB)[n]).rearrange("p (j d) -> p j d", d=D), AX.X, ALU.max,
                                negate=True).then_inc(nmax_ready, 1)

            def scale_keys(line, t, l):
                def wide(x):
                    return x.unsqueeze(2).broadcast_to([P, H, D])

                dve.wait_ge(tb_ready, al(t, l, 1, 1))
                line.did(v.tensor_scalar(beta[:, :], tb[:, :], 0.5, 0.5, ALU.mult, ALU.add))
                dve.wait_ge(e_ready, al(t, l, 2 * H, H))
                line.did(v.reciprocal(rsum[:, H:2 * H], esum[:, H:2 * H]))
                line.settle()
                line.did(v.tensor_tensor(rb[:, :], beta[:, :], rsum[:, H:2 * H], ALU.mult))
                line.settle()
                line.did(v.scalar_tensor_tensor(rrb[:, :], rb[:, :], -1.0, rsum[:, H:2 * H], ALU.mult, ALU.mult))
                line.settle()
                v.tensor_tensor(ekc[:, :, :], eqk[:, H:2 * H, :], wide(rrb[:, :]), ALU.mult).then_inc(ekc_ready, 1)
                dve.wait_ge(v_ready, al(t, l, 1, 1))
                v.tensor_tensor(rhs_v[l][:, :, :], bank(VB).rearrange("p (h d) -> p h d", d=D), wide(rb[:, :]),
                                ALU.mult).then_inc(rhs_ready, 1)

            def scale_queries(line, t, l):
                dve.wait_ge(e_ready, al(t, l, 2 * H, 2 * H))
                line.did(v.reciprocal(rsum[:, 0:H], esum[:, 0:H]))
                line.settle()
                v.tensor_tensor(eqk[:, 0:H, :], eqk[:, 0:H, :], rsum[:, 0:H].unsqueeze(2).broadcast_to([P, H, D]),
                                ALU.mult).then_inc(eq_ready, 1)

            def masks(m):
                return m.unsqueeze(1).broadcast_to([P, H // 2, P])

            def four(f, n):
                return bank(SOLVE[f][n]).rearrange("p (i q) -> p i q", i=H // 2)

            def move_scores(t, l):
                for f in range(2):
                    dve.wait_ge(moved_c[f], al(t, l, MOVED_C, C_U))
                    hold()
                    v.copy_predicated(t2t[f][:, :, :], masks(m1t), four(f, 0)).then_inc(moved_v[f], 1)
                    v.tensor_tensor(u8[f][:, :, :], four(f, 0), masks(mask_u8), ALU.mult).then_inc(moved_v[f], 1)
                for f in range(2):
                    dve.wait_ge(product[f], al(t, l, PRODUCTS, P_S))
                    v.tensor_tensor(s_m[f][:, :, :], four(f, 1), masks(mask_s), ALU.mult).then_inc(moved_v[f], 1)

            def move_masked(t, l, p, dst, n, m):
                for f in range(2):
                    dve.wait_ge(product[f], al(t, l, PRODUCTS, p))
                    hold()
                    v.copy_predicated(dst[f][:, :, :], masks(m), four(f, n)).then_inc(moved_v[f], 1)

            def add_right(t, l):
                for f in range(2):
                    dve.wait_ge(product[f], al(t, l, PRODUCTS, P_W))
                    r = rhs_v[l][:, H // 2 * f:H // 2 * (f + 1), :]
                    v.tensor_tensor(r, bank(SOLVE[f][0], 0, H // 2 * D).rearrange("p (i d) -> p i d", d=D), r,
                                    ALU.add).then_inc(moved_v[f], 1)

            def key_tops(t, q):
                c, lo = q // 2, 4 * (q % 2)
                dve.wait_ge(scores_ready, at(t, 4, q + 1))
                hold()
                src = bank(SCORE_BANK[q])
                for i in range(4):
                    second.did(v.max(best[:, c, lo + i, :], src[:, P * i:P * (i + 1)]))
                second.settle(alone=True)
                for i in range(4):
                    last = v.max_index(besti[:, c, lo + i, :], best[:, c, lo + i, :], src[:, P * i:P * (i + 1)])
                    if i < 3:
                        second.did(last)
                last.then_inc(scores_used, 1)

            def pair_tops(t):
                second.did(v.tensor_tensor(cand, best[:, 0, :, :].unsqueeze(3).broadcast_to([P, H, K, K]),
                                           best[:, 1, :, :].unsqueeze(2).broadcast_to([P, H, K, K]), ALU.add))
                dve.wait_ge(scores_used, at(t, 4, 4))
                second.did(v.tensor_copy(bestf[:, :, :, :], besti[:, :, :, :]))
                second.settle(alone=True)
                for h in range(H):
                    second.did(v.max(top[:, h, :], cand[:, h, :, :]))
                second.settle()
                v.tensor_tensor(shifted[:, :, :], top[:, :, :], top[:, :, 0:1].broadcast_to([P, H, K]),
                                ALU.subtract).then_inc(top_shifted, 1)
                for h in range(H):
                    second.did(v.max_index(topi[:, h, :], top[:, h, :], cand[:, h, :, :].rearrange("p a b -> p (a b)")))
                second.settle()
                flat = topi[:, :, :].rearrange("p h k -> p (h k)")
                second.did(v.tensor_scalar(pos[:, 0, :], flat, 3, None, ALU.logical_shift_right))
                second.did(v.tensor_scalar(pos[:, 1, :], flat, 7, None, ALU.bitwise_and))
                second.settle()
                second.did(v.tensor_copy(posf[:, :, :], pos[:, :, :]))
                second.settle()

            def pair_numbers(t):
                for c in range(2):
                    second.did(v.tensor_tensor(hot, posf[:, c, :].unsqueeze(2).broadcast_to([P, SLOTS, K]),
                                               iota8.unsqueeze(1).broadcast_to([P, SLOTS, K]), ALU.is_equal))
                    second.settle()
                    hot4 = hot.rearrange("p (h k) a -> p h k a", h=H)
                    second.did(v.tensor_tensor(hot4, hot4, bestf[:, c, :, :].unsqueeze(2).broadcast_to([P, H, K, K]),
                                               ALU.mult))
                    second.settle()
                    second.did(v.tensor_reduce(half_i[:, c, :], hot, AX.X, ALU.add))
                    second.settle()
                second.did(v.scalar_tensor_tensor(idx_next[:, :], half_i[:, 0, :], float(P), half_i[:, 1, :],
                                                  ALU.mult, ALU.add))
                second.settle()

            def weights(t):
                dve.wait_ge(top_exped, t + 1)
                second.did(v.tensor_reduce(w_sum[:, :], w_exp[:, :, :], AX.X, ALU.add))
                second.settle()
                second.did(v.reciprocal(w_rec[:, :], w_sum[:, :]))
                second.settle()
                second.did(v.scalar_tensor_tensor(w_next[:, :].rearrange("p (h k) -> p h k", h=H), w_exp[:, :, :], 0.5,
                                                  w_rec[:, :].unsqueeze(2).broadcast_to([P, H, K]),
                                                  ALU.mult, ALU.mult))
                second.settle()

            def dot(t, m):
                c = m * SP // CS
                dve.wait_ge(got[c], at(t, 16 * CS, 16 * CS))
                s = SP * m
                experts.did(v.tensor_tensor(prod[:, :, :], rows_got[:, s:s + SP, 0:P],
                                            q_now[:, :].unsqueeze(1).broadcast_to([P, SP, P]), ALU.mult))
                experts.settle()
                experts.did(v.tensor_reduce(xd[:, s - CS * c:s - CS * c + SP], prod[:, :, :], AX.X, ALU.add))
                experts.settle()

            def cube(t, c):
                experts.did(v.tensor_tensor(g1[:, :], xd[:, :], xd[:, :], ALU.mult))
                experts.settle()
                experts.did(v.tensor_scalar(g2[:, :], g1[:, :], 0.044715, 1.0, ALU.mult, ALU.add))
                experts.settle()
                v.tensor_tensor(g3[:, :], g2[:, :], xd[:, :], ALU.mult).then_inc(u_ready, 1)

            def gate(t, c):
                dve.wait_ge(th_ready, at(t, CHUNKS, c + 1))
                experts.did(v.scalar_tensor_tensor(g4[:, :], th[:, :], 1.0, xd[:, :], ALU.add, ALU.mult))
                experts.settle()
                v.tensor_tensor(val[:, CS * c:CS * (c + 1)], g4[:, :], w_now[:, CS * c:CS * (c + 1)],
                                ALU.mult).then_inc(val_ready, 1)

            def finish(t):
                dve.wait_ge(up_done, at(t, PARTS, PARTS))
                tile = (h_tok[:, t, :] if isinstance(t, int) else
                        h_tok[:, bass.ds(t, 1), :].rearrange("p t q -> p (t q)"))
                v.tensor_tensor(tile, bank(UP, 0, P), h_now[:, :], ALU.add).then_inc(out_ready, 1)

            def hand_over_indices(t, c):
                if c is not None:
                    for n in range(CHUNKS):
                        dve.wait_ge(got[n], at(c, 16 * CS, 16 * CS))
                v.tensor_copy(idx_now[:, :], idx_next[:, :]).then_inc(idx_ready, 1)

            def hand_over_query(t):
                second.did(v.tensor_copy(w_now[:, :], w_next[:, :]))
                second.did(v.tensor_copy(q_now[:, :], normed_s[:, :]))
                second.settle()

            def hand_over_residual(line, d):
                if d is not None:
                    dve.wait_ge(out_ready, d + 1)
                line.did(v.tensor_copy(h_now[:, :], h_s[:, :]))
                line.settle()

            def start_first(u):
                tile = h_tok[:, u, :] if isinstance(u, int) else h_tok[:, bass.ds(u, 1), :].rearrange("p t q -> p (t q)")
                first.start(u)
                first.did(v.tensor_tensor(h_f[:, :], tile, bias_sb[:, :], ALU.add))
                first.settle()
                layer_norm(first, 0, h_f[:, :])

            def project(u):
                dve.wait_ge(proj_ready, u + 1)
                v.tensor_tensor(xs[:, :], bank(4, 0, P), rows_sb[:, 0:P], ALU.add).then_inc(proj_used, 1)
                dve.wait_ge(proj_used, u + 1)

            def after_first(u):
                dve.wait_ge(att_ready, al(u, 0, 1, 1))
                first.did(v.tensor_tensor(xs[:, :], xs[:, :], bank(5, 0, P), ALU.add))
                first.settle()
                layer_norm(first, 2, xs[:, :])
                first.did(v.tensor_tensor(xs_b[:, :], xs[:, :], rows_sb[:, P:2 * P], ALU.add))
                first.settle()

            def end_first(u):
                dve.wait_ge(ff2_ready, u + 1)
                first.did(v.tensor_tensor(xs[:, :], xs_b[:, :], bank(5, 0, P), ALU.add))
                first.settle()

            def first_alone(u):
                start_first(u)
                project(u)
                layer_norm(first, 1, xs[:, :])
                maxima(u, 0, 0)
                maxima(u, 0, 1)
                scale_keys(first, u, 0)
                scale_queries(first, u, 0)
                move_scores(u, 0)
                move_masked(u, 0, P_A2, a2, 0, m2)
                move_masked(u, 0, P_A4, a4, 1, m4)
                add_right(u, 0)
                after_first(u)
                end_first(u)

            def step(t, u, c, d):
                second.start(t)
                if c is not None:
                    experts.start(c)
                layer_norm(second, 3, xs[:, :])
                second.did(v.tensor_tensor(res[:, :], xs[:, :], h_f[:, :], ALU.add))
                second.settle()
                maxima(t, 1, 0)
                maxima(t, 1, 1)
                if u is not None:
                    start_first(u)
                scale_keys(second, t, 1)
                scale_queries(second, t, 1)
                if u is not None:
                    project(u)
                if d is not None:
                    finish(d)
                if c is not None:
                    hand_over_residual(experts, d)
                    dot(c, 0)
                    dot(c, 1)
                    cube(c, 0)
                move_scores(t, 1)
                if c is not None:
                    gate(c, 0)
                move_masked(t, 1, P_A2, a2, 0, m2)
                if u is not None:
                    layer_norm(first, 1, xs[:, :])
                move_masked(t, 1, P_A4, a4, 1, m4)
                if u is not None:
                    maxima(u, 0, 0)
                    maxima(u, 0, 1)
                if c is not None:
                    dot(c, 2)
                add_right(t, 1)
                if u is not None:
                    scale_keys(first, u, 0)
                    scale_queries(first, u, 0)
                if c is not None:
                    dot(c, 3)
                    cube(c, 1)
                dve.wait_ge(att_ready, al(t, 1, 1, 1))
                second.did(v.tensor_tensor(h_s[:, :], res[:, :], bank(5, 0, P), ALU.add))
                second.settle()
                layer_norm(second, 4, h_s[:, :])
                if c is not None:
                    gate(c, 1)
                if u is not None:
                    move_scores(u, 0)
                key_tops(t, 0)
                if u is not None:
                    move_masked(u, 0, P_A2, a2, 0, m2)
                key_tops(t, 1)
                key_tops(t, 2)
                if u is not None:
                    move_masked(u, 0, P_A4, a4, 1, m4)
                key_tops(t, 3)
                pair_tops(t)
                if u is not None:
                    add_right(u, 0)
                if c is not None:
                    dot(c, 4)
                    dot(c, 5)
                    cube(c, 2)
                if u is not None:
                    after_first(u)
                if c is not None:
                    gate(c, 2)
                pair_numbers(t)
                weights(t)
                if u is not None:
                    end_first(u)
                if c is not None:
                    dot(c, 6)
                    dot(c, 7)
                    cube(c, 3)
                hand_over_indices(t, c)
                if c is not None:
                    gate(c, 3)
                    dve.wait_ge(val_ready, at(c, CHUNKS, CHUNKS))
                hand_over_query(t)

            first_alone(0)
            step(0, 1, None, None)
            second.a_tile = second.n
            step(1, 2, 0, None)
            with dve.Fori(2, TILES - 1) as t:
                step(t, t + 1, t - 1, t - 2)
            step(TILES - 1, None, TILES - 2, TILES - 3)
            experts.start(TILES - 1)
            finish(TILES - 2)
            hand_over_residual(experts, TILES - 2)
            for c in range(CHUNKS):
                dot(TILES - 1, 2 * c)
                dot(TILES - 1, 2 * c + 1)
                cube(TILES - 1, c)
                gate(TILES - 1, c)
            finish(TILES - 1)

        @block.tensor
        def _(pe):
            pe.wait_ge(x_landed, 16)
            for n in range(2 * WG):
                grp, half = n // 2, n % 2
                pe.wait_ge(masked, n + 1)
                w = ring[0:GP, n % RING, :].rearrange("p (e c q) -> p e c q", e=S // 2, c=CG)
                for k in range(CG):
                    c = CG * grp + k
                    for j in range(2):
                        last = nc.tensor.matmul(
                            bank(half)[B * j:B * (j + 1), :].rearrange("p (e q) -> p e q", e=S // 4),
                            x_sb[:, B * c:B * (c + 1)], w[:, S // 4 * j:S // 4 * (j + 1), k, :],
                            start=(c == 0), stop=(c == GC - 1))
                last.then_inc(w_used, 1)
                if grp == WG - 1:
                    pe.nop(nofuse=True)
                    nc.tensor.drain().then_inc(h_summed, 1)

            pe.wait_ge(mats_landed, 16)
            pe.wait_ge(consts_landed, 16 * (3 + P // S))
            mm = nc.tensor.matmul

            def turn_norm(t, n):
                pe.wait_ge(norm_ready[n], t + 1)
                nc.tensor.transpose(bank(NORM_BANK[n], 0, P), normed[n][:, :], ident).then_inc(norm_turned[n], 1)

            def project(t):
                pe.wait_ge(norm_moved[0], t + 1)
                mm(bank(4, 0, P), normed_t[0][:, :], mat("ip", 0), start=True, stop=True).then_inc(proj_ready, 1)

            def keys_values(t, l):
                n, w = (1, 3)[l], f"slow{l}"
                pe.wait_ge(norm_moved[n], t + 1)
                mm(bank(KB), normed_t[n][:, :], mat(w, 1, H * D), start=True, stop=True).then_inc(qk_ready, 1)
                mm(bank(QB, 0, H), normed_t[n][:, :], mats[:, OFF[w] + 3 * H * D:OFF[w] + QKV],
                   start=True, stop=True).then_inc(beta_ready, 1)
                mm(bank(VB), normed_t[n][:, :], mat(w, 2, H * D), start=True, stop=True).then_inc(v_ready, 1)

            def queries(t, l):
                n, w = (1, 3)[l], f"slow{l}"
                pe.wait_ge(tb_ready, al(t, l, 1, 1))
                mm(bank(QB), normed_t[n][:, :], mat(w, 0, H * D), start=True, stop=True).then_inc(qk_ready, 1)

            def turn_four(n, src, s):
                for i in range(HP):
                    last = nc.tensor.transpose(bank(n, P * i, P * (i + 1)), src[:, i, :], ident)
                last.then_inc(s, 1)

            pairs = eqk[:, :, :].rearrange("p (i f) d -> p i (f d)", f=2)

            def turn_keys(t, l):
                pe.wait_ge(e_ready, al(t, l, 2 * H, H))
                turn_four(KB, pairs[:, HP:2 * HP], ek_turned)

            def turn_rest(t, l):
                pe.wait_ge(ekc_ready, al(t, l, 1, 1))
                pe.wait_ge(rhs_ready, al(t, l, 1, 1))
                turn_four(VB, ekc[:, :, :].rearrange("p (i f) d -> p i (f d)", f=2), ekc_turned)
                pe.wait_ge(eq_ready, al(t, l, 1, 1))
                turn_four(QB, pairs[:, 0:HP], eq_turned)

            def scores(n, rhs, g):
                for i in range(2):
                    pair = 2 * g + i
                    last = mm(bank(SOLVE[g][n], 2 * P * i, 2 * P * (i + 1)), ek_t[:, pair, :],
                              rhs[:, pair, :, :].rearrange("p f q -> p (f q)"), start=True, stop=True)
                last.then_inc(product[g], 1)

            def multiply(g, n, lhs, rhs, w=P):
                for i in range(H // 2):
                    last = mm(bank(SOLVE[g][n], w * i, w * (i + 1)), lhs[:, i, :], rhs[:, i, :], start=True, stop=True)
                last.then_inc(product[g], 1)

            def key_scores(t, l):
                pe.wait_ge(ek_moved, al(t, l, 1, 1))
                pe.wait_ge(ekc_moved, al(t, l, 2, 2))
                for g in range(2):
                    scores(0, ekc_t, g)
                pe.wait_ge(eq_moved, al(t, l, 2, 2))
                for g in range(2):
                    scores(1, eq_t, g)

            def blocks_2(t, l):
                for g in range(2):
                    pe.wait_ge(moved_v[g], al(t, l, MOVED_V, V_U8))
                    for i in range(H // 2):
                        last = nc.tensor.transpose(bank(SOLVE[g][0], P * i, P * (i + 1)), t2t[g][:, i, :], ident)
                    last.then_inc(product[g], 1)
                for g in range(2):
                    pe.wait_ge(moved_c[g], al(t, l, MOVED_C, C_T2))
                    multiply(g, 0, u_raw[g], t2[g])

            def blocks_4(t, l):
                for f in range(2):
                    pe.wait_ge(moved_v[f], al(t, l, MOVED_V, V_A2))
                    multiply(f, 1, t2t[f], a2[f])
                    multiply(f, 0, a2[f], t2t[f])

            def blocks_4_off(t, l):
                for f in range(2):
                    pe.wait_ge(moved_c[f], al(t, l, MOVED_C, C_T4))
                    multiply(f, 1, u_raw[f], t4[f])

            def blocks_8(t, l):
                for f in range(2):
                    pe.wait_ge(moved_c[f], al(t, l, MOVED_C, C_T4T))
                    pe.wait_ge(moved_v[f], al(t, l, MOVED_V, V_A4))
                    multiply(f, 0, a4[f], t4t[f])

            def right_side(l, g):
                return rhs_v[l][:, H // 2 * g:H // 2 * (g + 1), :]

            def solve_first(t, l):
                for f in range(2):
                    pe.wait_ge(moved_c[f], al(t, l, MOVED_C, C_T8T))
                    multiply(f, 1, t8t[f], right_side(l, f), D)

            def solve_off(t, l):
                for f in range(2):
                    pe.wait_ge(moved_c[f], al(t, l, MOVED_C, C_Y))
                    multiply(f, 0, u8[f], y[f], D)

            def solve_last(t, l):
                for f in range(2):
                    pe.wait_ge(moved_v[f], al(t, l, MOVED_V, V_R))
                    multiply(f, 1, t8t[f], right_side(l, f), D)

            def outputs(t, l):
                for f in range(2):
                    pe.wait_ge(moved_c[f], al(t, l, MOVED_C, C_Z))
                    pe.nop(nofuse=True)
                    for j in range(H // 2):
                        i, row = (H // 2 * f + j) // 2, D * (j % 2)
                        last = mm(bank(3)[row:row + D, P * i:P * (i + 1)], z[f][:, j, :], s_m[f][:, j, :],
                                  start=True, stop=True)
                last.then_inc(o_ready, 1)

            def project_out(t, l):
                pe.wait_ge(o_moved, al(t, l, 1, 1))
                for i in range(HP):
                    last = mm(bank(5, 0, P), o_t[:, i, :], mat(f"out{l}", i), start=(i == 0), stop=(i == HP - 1))
                last.then_inc(att_ready, 1)

            def feed_in(t):
                pe.wait_ge(norm_moved[2], t + 1)
                for n in range(FC):
                    last = mm(bank(4, P * n, P * (n + 1)), mat("w1", n), normed_t[2][:, :], start=True, stop=True)
                last.then_inc(ff1_ready, 1)

            def feed_out(t):
                for n in range(FC):
                    pe.wait_ge(ff1_moved, at(t, FC, n + 1))
                    last = mm(bank(5, 0, P), ff[:, n, :], mat("w2", n), start=(n == 0), stop=(n == FC - 1))
                last.then_inc(ff2_ready, 1)

            def product_queries(t):
                pe.wait_ge(norm_moved[4], t + 1)
                for h in range(H):
                    last = mm(ps[:, P * h:P * (h + 1)], mat("wq", h), normed_t[4][:, :], start=True, stop=True)
                last.then_inc(qh_ready, 1)

            def key_products(t, q):
                c, lo = q // 2, 4 * (q % 2)
                pe.wait_ge(qh_moved, at(t, H, H))
                if q == 3:
                    pe.wait_ge(scores_used, at(t, 4, 1))
                for i in range(4):
                    h = lo + i
                    last = mm(bank(SCORE_BANK[q], P * i, P * (i + 1)), qh_t[D * c:D * (c + 1), h, :],
                              mat("keys", h)[D * c:D * (c + 1), :], start=True, stop=True)
                last.then_inc(scores_ready, 1)

            def up(t, m):
                pe.wait_ge(diag_ready, at(t, PARTS, m + 1))
                for k in range(SP):
                    s = SP * m + k
                    last = mm(bank(UP, 0, P), diag[:, m % 2, k, :], rows_got[:, s, P:2 * P],
                              start=(s == 0), stop=(s == SLOTS - 1))
                last.then_inc(up_done, 1)

            def nothing(*_):
                pass

            def first_alone(u):
                turn_norm(u, 0)
                project(u)
                turn_norm(u, 1)
                keys_values(u, 0)
                queries(u, 0)
                turn_keys(u, 0)
                turn_rest(u, 0)
                pe.wait_ge(proj_used, u + 1)
                key_scores(u, 0)
                blocks_2(u, 0)
                blocks_4(u, 0)
                blocks_4_off(u, 0)
                blocks_8(u, 0)
                solve_first(u, 0)
                solve_off(u, 0)
                solve_last(u, 0)
                outputs(u, 0)
                project_out(u, 0)
                turn_norm(u, 2)
                feed_in(u)
                feed_out(u)

            def step(t, u, c, d):
                if d is not None:
                    up(d, 6)
                    up(d, 7)
                turn_norm(t, 3)
                keys_values(t, 1)
                queries(t, 1)
                turn_keys(t, 1)
                if u is not None:
                    turn_norm(u, 0)
                    project(u)
                turn_rest(t, 1)
                if u is not None:
                    pe.wait_ge(proj_used, u + 1)
                key_scores(t, 1)
                blocks_2(t, 1)
                if c is not None:
                    if d is not None:
                        pe.wait_ge(out_ready, d + 1)
                    up(c, 0)
                blocks_4(t, 1)
                blocks_4_off(t, 1)
                if u is not None:
                    turn_norm(u, 1)
                    keys_values(u, 0)
                if c is not None:
                    up(c, 1)
                blocks_8(t, 1)
                if u is not None:
                    queries(u, 0)
                solve_first(t, 1)
                solve_off(t, 1)
                if u is not None:
                    turn_keys(u, 0)
                solve_last(t, 1)
                outputs(t, 1)
                project_out(t, 1)
                if u is not None:
                    turn_rest(u, 0)
                turn_norm(t, 4)
                if u is not None:
                    pe.wait_ge(norm_moved[4], t + 1)
                    key_scores(u, 0)
                if c is not None:
                    up(c, 2)
                product_queries(t)
                if u is not None:
                    blocks_2(u, 0)
                key_products(t, 0)
                key_products(t, 1)
                key_products(t, 2)
                if u is not None:
                    blocks_4(u, 0)
                if c is not None:
                    up(c, 3)
                if u is not None:
                    blocks_4_off(u, 0)
                key_products(t, 3)
                if u is not None:
                    blocks_8(u, 0)
                    solve_first(u, 0)
                    solve_off(u, 0)
                    solve_last(u, 0)
                    outputs(u, 0)
                    project_out(u, 0)
                if c is not None:
                    up(c, 4)
                if u is not None:
                    turn_norm(u, 2)
                    feed_in(u)
                    feed_out(u)
                if c is not None:
                    up(c, 5)

            first_alone(0)
            step(0, 1, None, None)
            step(1, 2, 0, None)
            with pe.Fori(2, TILES - 1) as t:
                step(t, t + 1, t - 1, t - 2)
            step(TILES - 1, None, TILES - 2, TILES - 3)
            up(TILES - 2, 6)
            up(TILES - 2, 7)
            pe.wait_ge(out_ready, TILES - 1)
            for m in range(PARTS):
                up(TILES - 1, m)


def constants():
    i = np.arange(P)
    row, col = i[:, None], i[None, :]
    same = row // S == col // S

    def off_diagonal(n):
        return (row // (2 * n) == col // (2 * n)) & (row // n % 2 == 1) & (col // n % 2 == 0)

    f = np.concatenate([np.eye(P), off_diagonal(8).T, same & (row <= col), np.tile(np.arange(K), (P, 1))], axis=1)
    m = np.concatenate([off_diagonal(1).T, off_diagonal(2), off_diagonal(4)], axis=1)
    return f.astype(np.float32), m.astype(np.int32)


def kernel(x, L0_tok_weight, L0_tok_bias, L0_tok_mask, L0_attn_ip_w, L0_attn_ip_b, L0_attn_fw_ln_g, L0_attn_fw_ln_b,
           L0_attn_fw_slow_w, L0_attn_fw_out_w, L0_attn_ff_ln_g, L0_attn_ff_ln_b, L0_attn_ff_w1, L0_attn_ff_b1,
           L0_attn_ff_w2, L0_attn_ff_b2, L0_ffn_Wq, L0_ffn_bq, L0_ffn_keys, L0_ffn_w_down_embed, L0_ffn_w_up_embed):
    import concourse.bacc as bacc
    from concourse.bass_utils import run_bass_kernel_spmd

    def slow(w):
        w = np.asarray(w).reshape(H, 3 * D + 1, P)
        parts = [w[:, D * n:D * (n + 1)].reshape(H * D, P) for n in range(3)] + [w[:, 3 * D]]
        return np.concatenate(parts, axis=0).T

    def chunked(w):
        w = np.asarray(w)
        return w.reshape(w.shape[0], -1, P).transpose(2, 1, 0).reshape(P, -1)

    def column(v):
        return np.asarray(v).reshape(-1, P).T

    packed = np.concatenate([
        np.asarray(L0_attn_ip_w).T, slow(L0_attn_fw_slow_w[0]), slow(L0_attn_fw_slow_w[1]),
        chunked(L0_attn_fw_out_w[0]), chunked(L0_attn_fw_out_w[1]),
        np.asarray(L0_attn_ff_w1).T, chunked(L0_attn_ff_w2), np.asarray(L0_ffn_Wq).T,
        np.asarray(L0_ffn_keys).transpose(1, 3, 0, 2).reshape(P, H * P),
        column(L0_attn_fw_ln_g[0]), column(L0_attn_fw_ln_b[0]), column(L0_attn_fw_ln_g[1]), column(L0_attn_fw_ln_b[1]),
        column(L0_attn_ff_ln_g), column(L0_attn_ff_ln_b), column(L0_attn_ff_b1), column(L0_ffn_bq)], axis=1)
    assert packed.shape == (P, PACKED)
    fconst, iconst = constants()
    arrays = {
        "weight": np.asarray(L0_tok_weight),
        "x_t": np.asarray(x).T.reshape(GP, GC * B),
        "mask": np.asarray(L0_tok_mask),
        "packed": packed,
        "bias": np.asarray(L0_tok_bias),
        "rows": np.concatenate([np.asarray(L0_attn_ip_b), np.asarray(L0_attn_ff_b2)]),
        "fconst": fconst,
        "iconst": iconst,
        "table": np.concatenate([np.asarray(L0_ffn_w_down_embed), np.asarray(L0_ffn_w_up_embed)], axis=1),
    }
    nc = bacc.Bacc("TRN2", target_bir_lowering=False, num_devices=1)
    arrays = {k: np.ascontiguousarray(a) for k, a in arrays.items()}
    args = [nc.dram_tensor(k, a.shape, mybir.dt.from_np(a.dtype), kind="ExternalInput").ap() for k, a in arrays.items()]
    h_dram = nc.dram_tensor("h_dram", (B, S, P), F32, kind="Internal").ap()
    out = nc.dram_tensor("out", (B, S, P), F32, kind="ExternalOutput").ap()
    build(nc, *args, h_dram, out)
    r = run_bass_kernel_spmd(nc, [arrays], core_ids=[0])
    return r.results[0]["out"]
```

```python
from contextlib import ExitStack

import numpy as np
import concourse.bass as bass
from concourse import mybir

F32 = mybir.dt.float32
U32 = mybir.dt.uint32
I32 = mybir.dt.int32
ALU = mybir.AluOpType
ACT = mybir.ActivationFunctionType
AX = mybir.AxisListType

B, G = 64, 5000
S, P = 16, 128
H, D = 8, 64
HP = H // 2
FC = 4
K = 8
SLOTS = H * K
TILES = B * S // P
GP = 125
GC = G // GP
CG = 4
WG = GC // CG
RING = 4
EPS = 1e-5

QKV = 3 * H * D + H
OFF = {}
_at = 0
for _name, _n in (("ip", P), ("slow0", QKV),
                  ("g0", 1), ("b0", 1), ("g1", 1), ("b1", 1), ("gf", 1), ("bf", 1), ("fb1", FC), ("bq", H),
                  ("out0", HP * P), ("w1", FC * P), ("w2", FC * P), ("slow1", QKV), ("out1", HP * P),
                  ("wq", H * P), ("keys", H * P)):
    OFF[_name] = _at
    _at += _n
PACKED = _at
EARLY = OFF["out0"]

(P_U, P_S, P_T2, P_A2, P_T4, P_T4T, P_A4, P_T8T, P_Y, P_W, P_Z) = range(1, 12)
PRODUCTS = 11
(V_T2T, V_U8, V_S, V_A2, V_A4, V_R) = range(1, 7)
MOVED_V = 6
(C_U, C_T2, C_T4, C_T4T, C_T8T, C_Y, C_Z) = range(1, 8)
MOVED_C = 7
NORMS = 5
CHUNKS = 4
CS = SLOTS // CHUNKS
PARTS = 8
SP = SLOTS // PARTS


def build(nc, weight, x_t, mask, packed, bias, rows, fconst, iconst, table, h_dram, out):
    with ExitStack() as ctx:
        def sb(name, shape, dt=F32):
            return ctx.enter_context(nc.sbuf_tensor(name, shape, dt))

        def sem(name):
            return ctx.enter_context(nc.semaphore(name))

        mats = sb("mats", [P, PACKED])
        bias_sb = sb("bias_sb", [P, P])
        rows_sb = sb("rows_sb", [P, 2 * P])
        fc_sb = sb("fc_sb", [P, 3 * P + K])
        ic_sb = sb("ic_sb", [P, 3 * P], I32)
        mask_mem = sb("mask_mem", [P, GC * P])
        x_mem = sb("x_mem", [P, GC * B])
        mask_sb, x_sb = mask_mem[0:GP, :], x_mem[0:GP, :]
        ring = sb("ring", [P, RING, S // 2 * CG * P])
        rows_got = ring[:, :, :].rearrange("p r (s n) -> p (r s) n", n=2 * P)
        h_cols = sb("h_cols", [P, 2, 512])
        h_tok = sb("h_tok", [P, TILES, P])
        ident = fc_sb[:, 0:P]
        mask_u8 = fc_sb[:, P:2 * P]
        mask_s = fc_sb[:, 2 * P:3 * P]
        iota8 = fc_sb[:, 3 * P:3 * P + K]
        m1t, m2, m4 = (ic_sb[:, P * n:P * (n + 1)] for n in range(3))

        def mat(name, n, w=P):
            return mats[:, OFF[name] + n * w:OFF[name] + (n + 1) * w]

        norm_scratch = [[sb(f"{name}{n}", [P, w])[:, :] for name, w in (
            ("stats", 6), ("mv", 2), ("var", 1), ("var2", 1), ("rs", 1), ("rs2", 1))] for n in range(2)]
        normed_f, normed_s, normed_ft, normed_st = (sb(name, [P, P])[:, :] for name in
                                                    ("normed_f", "normed_s", "normed_ft", "normed_st"))
        normed_m, normed_mt, xs_m, xs_b = (mask_mem[:, SP * P + P * n:SP * P + P * (n + 1)] for n in range(4))
        normed = [normed_f, normed_f, normed_m, normed_m, normed_s]
        normed_t = [normed_ft, normed_ft, normed_mt, normed_mt, normed_st]
        xs = sb("xs", [P, P])
        res = sb("res", [P, P])
        ff = x_mem[:, (H + HP) * P:(H + HP + FC) * P].rearrange("p (n q) -> p n q", n=FC)
        nmax = sb("nmax", [P, 2 * H])
        esum = sb("esum", [P, 2 * H])
        rsum = sb("rsum", [P, 2 * H])
        tb = sb("tb", [P, H])
        beta = sb("beta", [P, H])
        rb = sb("rb", [P, H])
        rrb = sb("rrb", [P, H])
        eqk = sb("eqk", [P, 2 * H, D])
        ekc = sb("ekc", [P, H, D])
        rhs_v = [sb(f"rhs_v{n}", [P, H, D]) for n in range(2)]
        ek_t = h_cols[:, 0, :].rearrange("p (i q) -> p i q", i=HP)
        ekc_t = sb("ekc_t", [P, HP, 2, P])
        eq_t = sb("eq_t", [P, HP, 2, P])

        def halves(name, width=P):
            return [sb(f"{name}{g}", [P, H // 2, width]) for g in range(2)]

        u_raw, u8, s_m = halves("u_raw"), halves("u8"), halves("s_m")
        t2, t2t, a2, a4 = halves("t2_"), halves("t2t_"), halves("a2_"), halves("a4_")
        t4, t4t, t8t = halves("t4_"), halves("t4t_"), halves("t8t_")
        y = halves("y", D)
        z = y
        o_t = x_mem[:, H * P:H * P + HP * P].rearrange("p (i q) -> p i q", i=HP)
        qh_t = x_mem[:, 0:H * P].rearrange("p (h q) -> p h q", h=H)
        best = sb("best", [P, 2, H, K])
        besti = sb("besti", [P, 2, H, K], U32)
        bestf = sb("bestf", [P, 2, H, K])
        top = sb("top", [P, H, K])
        topi = sb("topi", [P, H, K], U32)
        pos = sb("pos", [P, 2, SLOTS], U32)
        posf = sb("posf", [P, 2, SLOTS])
        half_i = sb("half_i", [P, 2, SLOTS])
        shifted = sb("shifted", [P, H, K])
        w_exp = sb("w_exp", [P, H, K])
        w_sum = sb("w_sum", [P, H])
        w_rec = sb("w_rec", [P, H])
        w_now = sb("w_now", [P, SLOTS])
        idx_all = sb("idx_all", [P, TILES, SLOTS], U32)
        idx_now = sb("idx_now", [P, 2, SLOTS], U32)
        q_now = sb("q_now", [P, P])
        prod = mask_mem[:, 0:SP * P].rearrange("p (s q) -> p s q", s=SP)
        xd = sb("xd", [P, CS])
        g1, g2 = sb("g1_", [P, CS]), sb("g2_", [P, CS])
        g3, g4 = sb("g3_", [P, CS]), sb("g4_", [P, CS])
        th = sb("th", [P, CS])
        val = sb("val", [P, SLOTS])
        diag = mask_mem[:, CS * P:2 * CS * P].rearrange("p (b s q) -> p b s q", b=2, s=SP)
        cand = mask_mem[:, 2 * CS * P:2 * CS * P + H * K * K].rearrange("p (h a b) -> p h a b", h=H, a=K)
        hot = mask_mem[:, 2 * CS * P + H * K * K:2 * CS * P + 2 * H * K * K].rearrange("p (s a) -> p s a", a=K)

        ps = ctx.enter_context(nc.psum_tensor("ps", [P, 8 * 512], F32))

        def bank(n, lo=0, hi=512):
            return ps[:, 512 * n + lo:512 * n + hi]

        QB, KB, VB = 1, 0, 2
        SOLVE = ((3, 4), (5, 6))
        UP = 7
        NORM_BANK = (1, 2, 0, 2, 0)
        SCORE_BANK = (2, 0, 1, 2)

        w_landed = [sem(f"w_landed{n}") for n in range(RING)]
        x_landed, mask_landed, mats_landed = sem("x_landed"), sem("mask_landed"), sem("mats_landed")
        consts_landed, late_landed = sem("consts_landed"), sem("late_landed")
        masked, w_used, h_summed, h_copied = sem("masked"), sem("w_used"), sem("h_summed"), sem("h_copied")
        h_stored, h_loaded = sem("h_stored"), sem("h_loaded")
        f_done, m_done, s_done, p_done, c_done, d_done = (sem(f"{name}_done") for name in "fmspcd")
        setup_done = sem("setup_done")
        norm_ready = [sem(f"norm_ready{n}") for n in range(NORMS)]
        norm_turned = [sem(f"norm_turned{n}") for n in range(NORMS)]
        norm_moved = [sem(f"norm_moved{n}") for n in range(NORMS)]
        proj_ready = sem("proj_ready")
        (qk_ready, v_ready, beta_ready, tb_ready, nmax_ready, e_ready, eq_ready, ekc_ready, rhs_ready, ek_turned,
         eq_turned, ekc_turned, ek_moved, eq_moved, ekc_moved, o_ready, o_moved, att_ready) = (
            [sem(f"{name}{n}") for n in range(2)] for name in (
                "qk_ready", "v_ready", "beta_ready", "tb_ready", "nmax_ready", "e_ready", "eq_ready", "ekc_ready",
                "rhs_ready", "ek_turned", "eq_turned", "ekc_turned", "ek_moved", "eq_moved", "ekc_moved", "o_ready",
                "o_moved", "att_ready"))
        product, moved_v, moved_c = ([[sem(f"{name}{n}{g}") for g in range(2)] for n in range(2)]
                                     for name in ("product", "moved_v", "moved_c"))
        scores_used = sem("scores_used")
        idx_copied = sem("idx_copied")
        att_used, biased, block_added = sem("att_used"), sem("biased"), sem("block_added")
        ff1_ready, ff1_moved, ff2_ready = sem("ff1_ready"), sem("ff1_moved"), sem("ff2_ready")
        qh_ready, qh_moved, scores_ready = sem("qh_ready"), sem("qh_moved"), sem("scores_ready")
        top_shifted, top_exped, idx_ready = sem("top_shifted"), sem("top_exped"), sem("idx_ready")
        got = [sem(f"got{n}") for n in range(PARTS)]
        u_ready, th_ready, val_ready, diag_ready, up_done = (sem("u_ready"), sem("th_ready"), sem("val_ready"),
                                                             sem("diag_ready"), sem("up_done"))
        out_ready, out_stored = sem("out_ready"), sem("out_stored")

        def at(t, a_tile, n):
            return t * a_tile + n

        def idx_tile(t):
            if isinstance(t, int):
                return idx_all[:, t, :]
            return idx_all[:, bass.ds(t, 1), :].rearrange("p t s -> p (t s)")

        block = ctx.enter_context(nc.Block())

        @block.sync
        def _(sp):
            sp.dma_start(x_sb[:, :], x_t).then_inc(x_landed, 16)
            w_view = weight.rearrange("e (p c) q -> p e (c q)", p=GP)
            sp.dma_start(mask_sb, mask.rearrange("(p c) q -> p (c q)", p=GP)).then_inc(mask_landed, 16)
            for n in range(2 * WG):
                grp, half = n // 2, n % 2
                if n >= RING:
                    sp.wait_ge(w_used, n - RING + 1)
                sp.dma_start(ring[0:GP, n % RING, :].rearrange("p (e k) -> p e k", e=S // 2),
                             w_view[:, S // 2 * half:S // 2 * (half + 1), CG * P * grp:CG * P * (grp + 1)]
                             ).then_inc(w_landed[n % RING], 16)
            h_view = h_dram.rearrange("b (f j i) q -> j b f (i q)", f=2, j=2)
            sp.wait_ge(h_copied, 2)
            for j in range(2):
                sp.dma_start(h_view[j], h_cols[B * j:B * (j + 1), :, :]).then_inc(h_stored, 16)
            sp.wait_ge(h_stored, 32)
            sp.dma_start(h_tok[:, :, :], h_dram.rearrange("(t a) e q -> (a e) t q", t=TILES)).then_inc(h_loaded, 16)
            out_view = out.rearrange("(t a) e q -> t (a e) q", t=TILES)
            with sp.Fori(0, TILES) as t:
                sp.wait_ge(out_ready, t + 1)
                sp.dma_start(out_view[bass.ds(t, 1), :, :].rearrange("t p q -> p (t q)"),
                             h_tok[:, bass.ds(t, 1), :].rearrange("p t q -> p (t q)")).then_inc(out_stored, 16)
            sp.wait_ge(out_stored, 16 * TILES)

        @block.gpsimd
        def _(pool):
            def gather(t, n, started=True):
                pool.wait_ge(idx_ready, t + 1)
                if started:
                    for m in range(PARTS):
                        pool.wait_ge(got[m], at(t - 2, 16 * SP, 16 * SP))
                pool.tensor_copy(idx_now[:, n, :], idx_tile(t)).then_inc(idx_copied, 1)
                pool.wait_ge(idx_copied, t + 1)
                pool.nop(nofuse=True)
                for c in range(CHUNKS):
                    if started or n == 1:
                        pool.wait_ge(up_done, at(t, PARTS, 2 * (c + 1) - PARTS))
                        pool.nop(nofuse=True)
                    for s in range(CS * c, CS * (c + 1)):
                        pool.indirect_dma_start(
                            out=rows_got[:, s, :], out_offset=None, in_=table,
                            in_offset=bass.IndirectOffsetOnAxis(ap=idx_now[:, n, s:s + 1], axis=0)
                        ).then_inc(got[s // SP], 16)

            gather(0, 0, started=False)
            gather(1, 1, started=False)
            with pool.Fori(1, TILES // 2) as pair:
                gather(2 * pair, 0)
                gather(2 * pair + 1, 1)

        @block.scalar
        def _(act):
            act.wait_ge(w_used, RING)
            act.dma_start(fc_sb[:, :], fconst).then_inc(consts_landed, 16)
            act.dma_start(ic_sb[:, :], iconst).then_inc(consts_landed, 16)
            for n in range(P // S):
                act.dma_start(bias_sb[S * n:S * (n + 1), :], bias).then_inc(consts_landed, 16)
            act.dma_start(rows_sb[:, :], rows.partition_broadcast(P)).then_inc(consts_landed, 16)
            act.wait_ge(w_used, 2 * WG - RING)
            act.dma_start(mats[:, 0:EARLY], packed[:, 0:EARLY]).then_inc(mats_landed, 16)
            act.wait_ge(consts_landed, 16 * (3 + P // S))
            act.wait_ge(mats_landed, 16)
            for f in range(2):
                act.wait_ge(h_summed, f + 1)
                nc.scalar.activation(h_cols[:, f, :], bank(f), ACT.Copy).then_inc(h_copied, 1)
            act.wait_ge(h_loaded, 16)
            act.dma_start(mats[:, EARLY:PACKED], packed[:, EARLY:PACKED]).then_inc(late_landed, 16)

            AFFINE = (None, ("g0", "b0"), ("gf", "bf"), ("g1", "b1"), None)

            def move_norm(t, n):
                act.wait_ge(norm_turned[n], t + 1)
                src = bank(NORM_BANK[n], 0, P)
                if AFFINE[n] is None:
                    nc.scalar.activation(normed_t[n], src, ACT.Copy).then_inc(norm_moved[n], 1)
                else:
                    g, b = AFFINE[n]
                    nc.scalar.activation(normed_t[n], src, ACT.Identity,
                                         bias=mat(b, 0, 1), scale=mat(g, 0, 1)).then_inc(norm_moved[n], 1)

            def beta(t, l):
                act.wait_ge(beta_ready[l], at(t, 1, 1))
                nc.scalar.activation(tb[:, :], bank(QB, 0, H), ACT.Tanh, scale=0.5).then_inc(tb_ready[l], 1)

            def exps(t, l, n):
                act.wait_ge(nmax_ready[l], at(t, 2, n + 1))
                for h in range(H):
                    j = (1 - n) * H + h
                    nc.scalar.activation(eqk[:, j, :], bank((KB, QB)[n], D * h, D * (h + 1)), ACT.Exp,
                                         bias=nmax[:, j:j + 1], accum_out=esum[:, j:j + 1]).then_inc(e_ready[l], 1)

            def move_keys(t, l):
                act.wait_ge(ek_turned[l], at(t, 1, 1))
                nc.scalar.activation(ek_t, bank(KB), ACT.Copy).then_inc(ek_moved[l], 1)

            def move_rest(t, l):
                def spread(dst, n, s):
                    for f in range(2):
                        rows = slice(D * f, D * (f + 1))
                        nc.scalar.activation(dst[rows, :, f, :], bank(n)[rows, :].rearrange("p (i q) -> p i q", i=HP),
                                             ACT.Copy).then_inc(s, 1)

                act.wait_ge(ekc_turned[l], at(t, 1, 1))
                spread(ekc_t, VB, ekc_moved[l])
                act.wait_ge(eq_turned[l], at(t, 1, 1))
                spread(eq_t, QB, eq_moved[l])

            def move(t, l, p, dst, n, width=P, halves=(0, 1)):
                for f in halves:
                    act.wait_ge(product[l][f], at(t, PRODUCTS, p))
                    nc.scalar.activation(dst[f][:, :, :], bank(SOLVE[f][n], 0, H // 2 * width),
                                         ACT.Copy).then_inc(moved_c[l][f], 1)

            def move_out(t, l):
                act.wait_ge(o_ready[l], at(t, 1, 1))
                nc.scalar.activation(o_t[:, :, :], bank(3), ACT.Copy).then_inc(o_moved[l], 1)

            def relu(t):
                act.wait_ge(ff1_ready, t + 1)
                for n in range(FC):
                    nc.scalar.activation(ff[:, n, :], bank(VB, P * n, P * (n + 1)), ACT.Relu,
                                         bias=mat("fb1", n, 1)).then_inc(ff1_moved, 1)

            def product_queries(t):
                act.wait_ge(qh_ready, t + 1)
                for h in range(H):
                    nc.scalar.activation(qh_t[:, h, :], ps[:, P * h:P * (h + 1)], ACT.Identity,
                                         bias=mat("bq", h, 1)).then_inc(qh_moved, 1)

            def top_exp(t):
                act.wait_ge(top_shifted, t + 1)
                nc.scalar.activation(w_exp[:, :, :], shifted[:, :, :], ACT.Exp).then_inc(top_exped, 1)

            def gelu(t, c, cols=slice(0, CS), n=None):
                act.wait_ge(u_ready, at(t, CHUNKS, (n or c) + 1))
                nc.scalar.activation(th[:, cols], g3[:, cols], ACT.Tanh, scale=0.7978845608028654).then_inc(th_ready, 1)

            def diagonals(t, m, n=None):
                act.wait_ge(val_ready, at(t, CHUNKS, (n or m * SP // CS) + 1))
                if m >= 2 or not isinstance(t, int) or t > 0:
                    act.wait_ge(up_done, at(t, PARTS, m - 1))
                for k in range(SP):
                    s = SP * m + k
                    last = nc.scalar.activation(diag[:, m % 2, k, :], ident, ACT.Copy, scale=val[:, s:s + 1])
                last.then_inc(diag_ready, 1)

            def step(f, m, t, c, d):
                if t is not None:
                    move(t, 1, P_U, u_raw, 0)
                if d is not None:
                    diagonals(d, 3)
                    diagonals(d, 4)
                if m is not None:
                    move_norm(m, 2)
                if t is not None:
                    move(t, 1, P_T2, t2, 0, halves=(0,))
                if f is not None:
                    move_norm(f, 0)
                if t is not None:
                    move(t, 1, P_T2, t2, 0, halves=(1,))
                if m is not None:
                    relu(m)
                if d is not None:
                    diagonals(d, 5)
                if t is not None:
                    move(t, 1, P_T4, t4, 1)
                    move(t, 1, P_T4T, t4t, 0)
                if f is not None:
                    move_norm(f, 1)
                if c is not None:
                    top_exp(c)
                if f is not None:
                    beta(f, 0)
                if t is not None:
                    move(t, 1, P_T8T, t8t, 0)
                    move(t, 1, P_Y, y, 1, D)
                if f is not None:
                    exps(f, 0, 0)
                    exps(f, 0, 1)
                if t is not None:
                    move(t, 1, P_Z, z, 1, D)
                    move_out(t, 1)
                if f is not None:
                    move_keys(f, 0)
                    move_rest(f, 0)
                if d is not None:
                    gelu(d, 3)
                if f is not None:
                    move(f, 0, P_U, u_raw, 0)
                if t is not None:
                    move_norm(t, 4)
                if m is not None:
                    move_norm(m, 3)
                if d is not None:
                    diagonals(d, 6)
                if f is not None:
                    move(f, 0, P_T2, t2, 0)
                if t is not None:
                    product_queries(t)
                if d is not None:
                    diagonals(d, 7)
                if c is not None:
                    gelu(c, 0)
                    diagonals(c, 0)
                if f is not None:
                    move(f, 0, P_T4, t4, 1)
                    move(f, 0, P_T4T, t4t, 0)
                if c is not None:
                    diagonals(c, 1)
                if f is not None:
                    move(f, 0, P_T8T, t8t, 0)
                    move(f, 0, P_Y, y, 1, D)
                if c is not None:
                    gelu(c, 1)
                if m is not None:
                    beta(m, 1)
                    exps(m, 1, 0)
                if f is not None:
                    move(f, 0, P_Z, z, 1, D)
                if m is not None:
                    exps(m, 1, 1)
                if f is not None:
                    move_out(f, 0)
                if m is not None:
                    move_keys(m, 1)
                if c is not None:
                    diagonals(c, 2)
                if m is not None:
                    move_rest(m, 1)
                if c is not None:
                    gelu(c, 2)

            step(0, None, None, None, None)
            step(1, 0, None, None, None)
            step(2, 1, 0, None, None)
            step(3, 2, 1, 0, None)
            with act.Fori(2, TILES - 2) as t:
                step(t + 2, t + 1, t, t - 1, t - 2)
            step(None, TILES - 1, TILES - 2, TILES - 3, TILES - 4)
            step(None, None, TILES - 1, TILES - 2, TILES - 3)
            top_exp(TILES - 1)
            for m in range(3, PARTS):
                if m == 6:
                    gelu(TILES - 2, 3)
                diagonals(TILES - 2, m)
            for c in range(CHUNKS - 1):
                gelu(TILES - 1, c)
                for m in range(2 * c, 2 * c + 2):
                    diagonals(TILES - 1, m)
            for n in range(2):
                gelu(TILES - 1, CHUNKS - 1, slice(SP * n, SP * (n + 1)), CHUNKS - 1 + n)
                diagonals(TILES - 1, PARTS - 2 + n, CHUNKS - 1 + n)

        @block.vector
        def _(dve):
            v = nc.vector

            class Line:

                def __init__(self, done, a_tile=None):
                    self.done, self.a_tile, self.t, self.n = done, a_tile, 0, 0

                def start(self, t):
                    if isinstance(self.t, int) and self.a_tile is None and self.n:
                        self.a_tile = self.n
                    assert self.n in (0, self.a_tile)
                    self.t, self.n = t, 0

                def did(self, instruction):
                    self.n += 1
                    return instruction.then_inc(self.done, 1)

                def settle(self, alone=False):
                    dve.wait_ge(self.done, at(self.t, self.a_tile, self.n) if self.a_tile else self.n)
                    if alone:
                        dve.nop(nofuse=True)

            first, middle, second = Line(f_done), Line(m_done), Line(s_done)
            chosen, experts = Line(p_done), Line(c_done)
            late = Line(d_done, 2 * SP + 2 + 1)

            def hold():
                dve.nop(nofuse=True)

            dve.wait_ge(mask_landed, 16)
            for n in range(2 * WG):
                grp = n // 2
                dve.wait_ge(w_landed[n % RING], 16 * (n // RING + 1))
                for k in range(0, CG, CG // 2):
                    w = ring[0:GP, n % RING, :].rearrange("p (e k) -> p e k", e=S // 2)[:, :, P * k:P * (k + CG // 2)]
                    m = mask_sb[:, P * (CG * grp + k):P * (CG * grp + k + CG // 2)]
                    v.tensor_tensor(w, w, m.unsqueeze(1).broadcast_to([GP, S // 2, CG // 2 * P]),
                                    ALU.mult).then_inc(masked, 1)
            dve.wait_ge(consts_landed, 16 * (3 + P // S))
            for dst in (ekc_t, eq_t):
                v.memset(dst[:, :, :, :], 0.0).then_inc(setup_done, 1)
            for dst in (*t2t, *a2, *a4):
                v.tensor_copy(dst[:, :, :], ident.unsqueeze(1).broadcast_to([P, HP, P])).then_inc(setup_done, 1)
            dve.wait_ge(setup_done, 8)
            dve.wait_ge(h_loaded, 16)
            v.tensor_tensor(h_tok[:, :, :], h_tok[:, :, :], bias_sb[:, :].unsqueeze(1).broadcast_to([P, TILES, P]),
                            ALU.add).then_inc(biased, 1)
            dve.wait_ge(biased, 1)
            dve.wait_ge(mats_landed, 16)

            def layer_norms(*norms):
                chains = [(*norm, scratch) for norm, scratch in zip(norms, norm_scratch) if norm is not None]

                def settle(alone=False):
                    for line, *_ in chains:
                        line.settle(alone)

                for line, n, src, (stats, mv, var, var2, rs, rs2) in chains:
                    line.did(v.bn_stats(stats, src))
                settle(alone=True)
                for line, n, src, (stats, mv, var, var2, rs, rs2) in chains:
                    line.did(v.bn_aggr(mv, stats))
                settle()
                for line, n, src, (stats, mv, var, var2, rs, rs2) in chains:
                    line.did(v.tensor_scalar(var, mv[:, 1:2], EPS, None, ALU.add))
                settle()
                for line, n, src, (stats, mv, var, var2, rs, rs2) in chains:
                    line.did(v.tensor_scalar(rs.bitcast(I32), var.bitcast(I32), -0.5, float(0x5F3759DF),
                                             ALU.mult, ALU.add))
                    line.did(v.tensor_scalar(var2, var, -0.5, None, ALU.mult))
                settle()
                for _ in range(3):
                    for line, n, src, (stats, mv, var, var2, rs, rs2) in chains:
                        line.did(v.scalar_tensor_tensor(rs2, rs, var2, rs, ALU.mult, ALU.mult))
                    settle()
                    for line, n, src, (stats, mv, var, var2, rs, rs2) in chains:
                        line.did(v.scalar_tensor_tensor(rs, rs2, 1.5, rs, ALU.add, ALU.mult))
                    settle()
                for line, n, src, (stats, mv, var, var2, rs, rs2) in chains:
                    v.tensor_scalar(normed[n], src, mv[:, 0:1], rs, ALU.subtract, ALU.mult).then_inc(norm_ready[n], 1)

            def maxima(t, l, n):
                j = (1 - n) * H
                dve.wait_ge(qk_ready[l], at(t, 2, n + 1))
                v.tensor_reduce(nmax[:, j:j + H], bank((KB, QB)[n]).rearrange("p (j d) -> p j d", d=D), AX.X, ALU.max,
                                negate=True).then_inc(nmax_ready[l], 1)

            def scale_keys(line, t, l):
                def wide(x):
                    return x.unsqueeze(2).broadcast_to([P, H, D])

                dve.wait_ge(tb_ready[l], at(t, 1, 1))
                line.did(v.tensor_scalar(beta[:, :], tb[:, :], 0.5, 0.5, ALU.mult, ALU.add))
                dve.wait_ge(e_ready[l], at(t, 2 * H, H))
                line.did(v.reciprocal(rsum[:, H:2 * H], esum[:, H:2 * H]))
                line.settle()
                line.did(v.tensor_tensor(rb[:, :], beta[:, :], rsum[:, H:2 * H], ALU.mult))
                line.settle()
                line.did(v.scalar_tensor_tensor(rrb[:, :], rb[:, :], -1.0, rsum[:, H:2 * H], ALU.mult, ALU.mult))
                line.settle()
                v.tensor_tensor(ekc[:, :, :], eqk[:, H:2 * H, :], wide(rrb[:, :]), ALU.mult).then_inc(ekc_ready[l], 1)
                dve.wait_ge(v_ready[l], at(t, 1, 1))
                v.tensor_tensor(rhs_v[l][:, :, :], bank(VB).rearrange("p (h d) -> p h d", d=D), wide(rb[:, :]),
                                ALU.mult).then_inc(rhs_ready[l], 1)

            def scale_queries(line, t, l):
                dve.wait_ge(e_ready[l], at(t, 2 * H, 2 * H))
                line.did(v.reciprocal(rsum[:, 0:H], esum[:, 0:H]))
                line.settle()
                v.tensor_tensor(eqk[:, 0:H, :], eqk[:, 0:H, :], rsum[:, 0:H].unsqueeze(2).broadcast_to([P, H, D]),
                                ALU.mult).then_inc(eq_ready[l], 1)

            def masks(m):
                return m.unsqueeze(1).broadcast_to([P, H // 2, P])

            def four(f, n):
                return bank(SOLVE[f][n]).rearrange("p (i q) -> p i q", i=H // 2)

            def move_scores(t, l, halves=(0, 1)):
                for f in halves:
                    dve.wait_ge(moved_c[l][f], at(t, MOVED_C, C_U))
                    hold()
                    v.copy_predicated(t2t[f][:, :, :], masks(m1t), four(f, 0)).then_inc(moved_v[l][f], 1)
                    v.tensor_tensor(u8[f][:, :, :], four(f, 0), masks(mask_u8), ALU.mult).then_inc(moved_v[l][f], 1)

            def move_outs(t, l, halves=(0, 1)):
                for f in halves:
                    dve.wait_ge(product[l][f], at(t, PRODUCTS, P_S))
                    v.tensor_tensor(s_m[f][:, :, :], four(f, 1), masks(mask_s), ALU.mult).then_inc(moved_v[l][f], 1)

            def move_masked(t, l, p, dst, n, m, halves=(0, 1)):
                for f in halves:
                    dve.wait_ge(product[l][f], at(t, PRODUCTS, p))
                    hold()
                    v.copy_predicated(dst[f][:, :, :], masks(m), four(f, n)).then_inc(moved_v[l][f], 1)

            def add_right(t, l, halves=(0, 1)):
                for f in halves:
                    dve.wait_ge(product[l][f], at(t, PRODUCTS, P_W))
                    r = rhs_v[l][:, H // 2 * f:H // 2 * (f + 1), :]
                    v.tensor_tensor(r, bank(SOLVE[f][0], 0, H // 2 * D).rearrange("p (i d) -> p i d", d=D), r,
                                    ALU.add).then_inc(moved_v[l][f], 1)

            def key_tops(t, q):
                c, lo = q // 2, 4 * (q % 2)
                dve.wait_ge(scores_ready, at(t, 4, q + 1))
                hold()
                src = bank(SCORE_BANK[q])
                for i in range(4):
                    second.did(v.max(best[:, c, lo + i, :], src[:, P * i:P * (i + 1)]))
                second.settle(alone=True)
                for i in range(4):
                    last = v.max_index(besti[:, c, lo + i, :], best[:, c, lo + i, :], src[:, P * i:P * (i + 1)])
                    if i < 3:
                        second.did(last)
                last.then_inc(scores_used, 1)

            def pair_tops(t):
                chosen.did(v.tensor_tensor(cand, best[:, 0, :, :].unsqueeze(3).broadcast_to([P, H, K, K]),
                                           best[:, 1, :, :].unsqueeze(2).broadcast_to([P, H, K, K]), ALU.add))
                dve.wait_ge(scores_used, at(t, 4, 4))
                chosen.did(v.tensor_copy(bestf[:, :, :, :], besti[:, :, :, :]))
                chosen.settle(alone=True)
                for h in range(H):
                    chosen.did(v.max(top[:, h, :], cand[:, h, :, :]))
                chosen.settle()
                v.tensor_tensor(shifted[:, :, :], top[:, :, :], top[:, :, 0:1].broadcast_to([P, H, K]),
                                ALU.subtract).then_inc(top_shifted, 1)
                for h in range(H):
                    chosen.did(v.max_index(topi[:, h, :], top[:, h, :], cand[:, h, :, :].rearrange("p a b -> p (a b)")))
                chosen.settle()
                flat = topi[:, :, :].rearrange("p h k -> p (h k)")
                chosen.did(v.tensor_scalar(pos[:, 0, :], flat, 3, None, ALU.logical_shift_right))
                chosen.did(v.tensor_scalar(pos[:, 1, :], flat, 7, None, ALU.bitwise_and))
                chosen.settle()
                chosen.did(v.tensor_copy(posf[:, :, :], pos[:, :, :]))
                chosen.settle()

            def pair_numbers(t):
                for c in range(2):
                    chosen.did(v.tensor_tensor(hot, posf[:, c, :].unsqueeze(2).broadcast_to([P, SLOTS, K]),
                                               iota8.unsqueeze(1).broadcast_to([P, SLOTS, K]), ALU.is_equal))
                    chosen.settle()
                    hot4 = hot.rearrange("p (h k) a -> p h k a", h=H)
                    chosen.did(v.tensor_tensor(hot4, hot4, bestf[:, c, :, :].unsqueeze(2).broadcast_to([P, H, K, K]),
                                               ALU.mult))
                    chosen.settle()
                    chosen.did(v.tensor_reduce(half_i[:, c, :], hot, AX.X, ALU.add))
                    chosen.settle()
                v.scalar_tensor_tensor(idx_tile(t), half_i[:, 0, :], float(P), half_i[:, 1, :],
                                       ALU.mult, ALU.add).then_inc(idx_ready, 1)

            def weights(t):
                dve.wait_ge(top_exped, t + 1)
                chosen.did(v.tensor_reduce(w_sum[:, :], w_exp[:, :, :], AX.X, ALU.add))
                chosen.settle()
                chosen.did(v.reciprocal(w_rec[:, :], w_sum[:, :]))
                chosen.settle()
                chosen.did(v.scalar_tensor_tensor(w_now[:, :].rearrange("p (h k) -> p h k", h=H), w_exp[:, :, :], 0.5,
                                                  w_rec[:, :].unsqueeze(2).broadcast_to([P, H, K]),
                                                  ALU.mult, ALU.mult))
                chosen.settle()

            def dot(line, t, m):
                c = m * SP // CS
                dve.wait_ge(got[m], at(t, 16 * SP, 16 * SP))
                for k in range(SP):
                    s = SP * m + k
                    line.did(v.scalar_tensor_tensor(prod[:, k, :], rows_got[:, s, 0:P], 1.0, q_now[:, :], ALU.mult,
                                                    ALU.mult, accum_out=xd[:, s - CS * c:s - CS * c + 1]))
                line.settle()

            def cube(line, c, cols=slice(0, CS)):
                line.did(v.tensor_tensor(g1[:, cols], xd[:, cols], xd[:, cols], ALU.mult))
                line.settle()
                line.did(v.tensor_scalar(g2[:, cols], g1[:, cols], 0.044715, 1.0, ALU.mult, ALU.add))
                line.settle()
                v.tensor_tensor(g3[:, cols], g2[:, cols], xd[:, cols], ALU.mult).then_inc(u_ready, 1)

            def gate(line, t, c, cols=slice(0, CS), n=None):
                dve.wait_ge(th_ready, at(t, CHUNKS, (n or c) + 1))
                line.did(v.scalar_tensor_tensor(g4[:, cols], th[:, cols], 1.0, xd[:, cols], ALU.add, ALU.mult))
                line.settle()
                slots = slice(CS * c + cols.start, CS * c + cols.stop)
                v.tensor_tensor(val[:, slots], g4[:, cols], w_now[:, slots], ALU.mult).then_inc(val_ready, 1)

            def tile_of(t):
                if isinstance(t, int):
                    return h_tok[:, t, :]
                return h_tok[:, bass.ds(t, 1), :].rearrange("p t q -> p (t q)")

            def finish(t):
                dve.wait_ge(up_done, at(t, PARTS, PARTS))
                v.tensor_tensor(tile_of(t), bank(UP, 0, P), tile_of(t), ALU.add).then_inc(out_ready, 1)

            def hand_over_query():
                experts.did(v.tensor_copy(q_now[:, :], normed_s))
                experts.settle()

            def add_second(t):
                dve.wait_ge(att_ready[1], at(t, 1, 1))
                v.tensor_tensor(tile_of(t), res[:, :], bank(5, 0, P), ALU.add).then_inc(block_added, 1)
                dve.wait_ge(block_added, t + 1)
                hold()

            def project(f):
                dve.wait_ge(proj_ready, f + 1)
                first.did(v.tensor_tensor(xs[:, :], bank(1, 0, P), rows_sb[:, 0:P], ALU.add))
                first.settle()

            def add_first(m):
                dve.wait_ge(att_ready[0], at(m, 1, 1))
                v.tensor_tensor(xs_m, xs[:, :], bank(5, 0, P), ALU.add).then_inc(att_used, 1)
                dve.wait_ge(att_used, m + 1)

            def end_feed(m):
                dve.wait_ge(ff2_ready, m + 1)
                middle.did(v.tensor_tensor(xs_m, xs_b, bank(0, 0, P), ALU.add))
                middle.settle()

            def step(f, m, t, c, d):
                for line, tile in ((first, f), (middle, m), (second, t), (chosen, c), (experts, c), (late, d)):
                    if tile is not None:
                        line.start(tile)
                layer_norms((middle, 2, xs_m) if m is not None else None,
                            (first, 0, tile_of(f)) if f is not None else None)
                if t is not None:
                    move_scores(t, 1)
                    move_outs(t, 1)
                if c is not None:
                    pair_tops(c)
                if t is not None:
                    move_masked(t, 1, P_A2, a2, 0, m2, halves=(0,))
                if m is not None:
                    middle.did(v.tensor_tensor(xs_b, xs_m, rows_sb[:, P:2 * P], ALU.add))
                    middle.settle()
                if t is not None:
                    move_masked(t, 1, P_A2, a2, 0, m2, halves=(1,))
                if f is not None:
                    project(f)
                if m is not None:
                    end_feed(m)
                if f is not None:
                    layer_norms((first, 1, xs[:, :]))
                if c is not None:
                    pair_numbers(c)
                if t is not None:
                    move_masked(t, 1, P_A4, a4, 1, m4)
                if f is not None:
                    maxima(f, 0, 0)
                if d is not None:
                    dot(late, d, 6)
                if f is not None:
                    maxima(f, 0, 1)
                if t is not None:
                    add_right(t, 1)
                if f is not None:
                    scale_keys(first, f, 0)
                    scale_queries(first, f, 0)
                if d is not None:
                    dot(late, d, 7)
                if c is not None:
                    hand_over_query()
                if d is not None:
                    cube(late, 3)
                if t is not None:
                    add_second(t)
                layer_norms((middle, 3, xs_m) if m is not None else None,
                            (second, 4, tile_of(t)) if t is not None else None)
                if d is not None:
                    gate(late, d, 3)
                    dve.wait_ge(val_ready, at(d, CHUNKS, CHUNKS))
                if c is not None:
                    weights(c)
                if f is not None:
                    move_scores(f, 0)
                    move_outs(f, 0, halves=(0,))
                if c is not None:
                    dot(experts, c, 0)
                if f is not None:
                    move_outs(f, 0, halves=(1,))
                if c is not None:
                    dot(experts, c, 1)
                    cube(experts, 0)
                if f is not None:
                    move_masked(f, 0, P_A2, a2, 0, m2)
                if c is not None:
                    gate(experts, c, 0)
                if m is not None:
                    middle.did(v.tensor_tensor(res[:, :], xs_m, tile_of(m), ALU.add))
                    middle.settle()
                if t is not None:
                    key_tops(t, 0)
                if d is not None:
                    finish(d)
                if t is not None:
                    key_tops(t, 1)
                if f is not None:
                    move_masked(f, 0, P_A4, a4, 1, m4)
                if t is not None:
                    key_tops(t, 2)
                    key_tops(t, 3)
                if c is not None:
                    dot(experts, c, 2)
                    dot(experts, c, 3)
                    cube(experts, 1)
                if f is not None:
                    add_right(f, 0)
                if c is not None:
                    gate(experts, c, 1)
                if m is not None:
                    maxima(m, 1, 0)
                    maxima(m, 1, 1)
                if c is not None:
                    dot(experts, c, 4)
                if m is not None:
                    scale_keys(middle, m, 1)
                    scale_queries(middle, m, 1)
                if f is not None:
                    add_first(f)
                if c is not None:
                    dot(experts, c, 5)
                    cube(experts, 2)
                    gate(experts, c, 2)

            step(0, None, None, None, None)
            step(1, 0, None, None, None)
            step(2, 1, 0, None, None)
            step(3, 2, 1, 0, None)
            with dve.Fori(2, TILES - 2) as t:
                step(t + 2, t + 1, t, t - 1, t - 2)
            step(None, TILES - 1, TILES - 2, TILES - 3, TILES - 4)
            step(None, None, TILES - 1, TILES - 2, TILES - 3)
            late.start(TILES - 2)
            experts.start(TILES - 1)
            chosen.start(TILES - 1)
            pair_tops(TILES - 1)
            pair_numbers(TILES - 1)
            dot(late, TILES - 2, 6)
            dot(late, TILES - 2, 7)
            cube(late, 3)
            gate(late, TILES - 2, 3)
            dve.wait_ge(val_ready, at(TILES - 2, CHUNKS, CHUNKS))
            weights(TILES - 1)
            hand_over_query()
            finish(TILES - 2)
            for c in range(CHUNKS - 1):
                dot(experts, TILES - 1, 2 * c)
                dot(experts, TILES - 1, 2 * c + 1)
                cube(experts, c)
                gate(experts, TILES - 1, c)
            late.start(TILES - 1)
            for n in range(2):
                cols = slice(SP * n, SP * (n + 1))
                dot(late, TILES - 1, PARTS - 2 + n)
                cube(late, CHUNKS - 1, cols)
                gate(late, TILES - 1, CHUNKS - 1, cols, CHUNKS - 1 + n)
            finish(TILES - 1)

        @block.tensor
        def _(pe):
            pe.wait_ge(x_landed, 16)
            for n in range(2 * WG):
                grp, half = n // 2, n % 2
                w = ring[0:GP, n % RING, :].rearrange("p (e c q) -> p e c q", e=S // 2, c=CG)
                for k in range(CG):
                    c = CG * grp + k
                    if k % (CG // 2) == 0:
                        pe.wait_ge(masked, 2 * n + k // (CG // 2) + 1)
                    for j in range(2):
                        last = nc.tensor.matmul(
                            bank(half)[B * j:B * (j + 1), :].rearrange("p (e q) -> p e q", e=S // 4),
                            x_sb[:, B * c:B * (c + 1)], w[:, S // 4 * j:S // 4 * (j + 1), k, :],
                            start=(c == 0), stop=(c == GC - 1))
                last.then_inc(w_used, 1)
                if grp == WG - 1:
                    pe.nop(nofuse=True)
                    nc.tensor.drain().then_inc(h_summed, 1)

            pe.wait_ge(mats_landed, 16)
            pe.wait_ge(consts_landed, 16 * (3 + P // S))
            mm = nc.tensor.matmul

            def turn_norm(t, n):
                pe.wait_ge(norm_ready[n], t + 1)
                nc.tensor.transpose(bank(NORM_BANK[n], 0, P), normed[n], ident).then_inc(norm_turned[n], 1)

            def project(t):
                pe.wait_ge(norm_moved[0], t + 1)
                mm(bank(1, 0, P), normed_t[0], mat("ip", 0), start=True, stop=True).then_inc(proj_ready, 1)

            def keys_values(t, l):
                n, w = (1, 3)[l], f"slow{l}"
                pe.wait_ge(norm_moved[n], t + 1)
                mm(bank(KB), normed_t[n], mat(w, 1, H * D), start=True, stop=True).then_inc(qk_ready[l], 1)
                mm(bank(QB, 0, H), normed_t[n], mats[:, OFF[w] + 3 * H * D:OFF[w] + QKV],
                   start=True, stop=True).then_inc(beta_ready[l], 1)
                mm(bank(VB), normed_t[n], mat(w, 2, H * D), start=True, stop=True).then_inc(v_ready[l], 1)

            def queries(t, l):
                n, w = (1, 3)[l], f"slow{l}"
                pe.wait_ge(tb_ready[l], at(t, 1, 1))
                mm(bank(QB), normed_t[n], mat(w, 0, H * D), start=True, stop=True).then_inc(qk_ready[l], 1)

            def turn_four(n, src, s):
                for i in range(HP):
                    last = nc.tensor.transpose(bank(n, P * i, P * (i + 1)), src[:, i, :], ident)
                last.then_inc(s, 1)

            pairs = eqk[:, :, :].rearrange("p (i f) d -> p i (f d)", f=2)

            def turn_keys(t, l):
                pe.wait_ge(e_ready[l], at(t, 2 * H, H))
                turn_four(KB, pairs[:, HP:2 * HP], ek_turned[l])

            def turn_rest(t, l):
                pe.wait_ge(ekc_ready[l], at(t, 1, 1))
                pe.wait_ge(rhs_ready[l], at(t, 1, 1))
                turn_four(VB, ekc[:, :, :].rearrange("p (i f) d -> p i (f d)", f=2), ekc_turned[l])
                pe.wait_ge(eq_ready[l], at(t, 1, 1))
                turn_four(QB, pairs[:, 0:HP], eq_turned[l])

            def scores(l, n, rhs, g):
                for i in range(2):
                    pair = 2 * g + i
                    last = mm(bank(SOLVE[g][n], 2 * P * i, 2 * P * (i + 1)), ek_t[:, pair, :],
                              rhs[:, pair, :, :].rearrange("p f q -> p (f q)"), start=True, stop=True)
                last.then_inc(product[l][g], 1)

            def multiply(l, g, n, lhs, rhs, w=P):
                for i in range(H // 2):
                    last = mm(bank(SOLVE[g][n], w * i, w * (i + 1)), lhs[:, i, :], rhs[:, i, :], start=True, stop=True)
                last.then_inc(product[l][g], 1)

            def key_scores(t, l, used=None):
                pe.wait_ge(ek_moved[l], at(t, 1, 1))
                pe.wait_ge(ekc_moved[l], at(t, 2, 2))
                scores(l, 0, ekc_t, 0)
                if used is not None:
                    pe.wait_ge(*used)
                scores(l, 0, ekc_t, 1)
                pe.wait_ge(eq_moved[l], at(t, 2, 2))
                for g in range(2):
                    scores(l, 1, eq_t, g)

            def turn_blocks(t, l, halves=(0, 1)):
                for g in halves:
                    pe.wait_ge(moved_v[l][g], at(t, MOVED_V, V_U8))
                    for i in range(H // 2):
                        last = nc.tensor.transpose(bank(SOLVE[g][0], P * i, P * (i + 1)), t2t[g][:, i, :], ident)
                    last.then_inc(product[l][g], 1)

            def blocks_2(t, l, halves=(0, 1)):
                for g in halves:
                    pe.wait_ge(moved_c[l][g], at(t, MOVED_C, C_T2))
                    multiply(l, g, 0, u_raw[g], t2[g])

            def blocks_4(t, l, halves=(0, 1)):
                for f in halves:
                    pe.wait_ge(moved_v[l][f], at(t, MOVED_V, V_A2))
                    multiply(l, f, 1, t2t[f], a2[f])
                    multiply(l, f, 0, a2[f], t2t[f])

            def blocks_4_off(t, l, halves=(0, 1)):
                for f in halves:
                    pe.wait_ge(moved_c[l][f], at(t, MOVED_C, C_T4))
                    multiply(l, f, 1, u_raw[f], t4[f])

            def blocks_8(t, l, halves=(0, 1)):
                for f in halves:
                    pe.wait_ge(moved_c[l][f], at(t, MOVED_C, C_T4T))
                    pe.wait_ge(moved_v[l][f], at(t, MOVED_V, V_A4))
                    multiply(l, f, 0, a4[f], t4t[f])

            def right_side(l, g):
                return rhs_v[l][:, H // 2 * g:H // 2 * (g + 1), :]

            def solve_first(t, l, halves=(0, 1)):
                for f in halves:
                    pe.wait_ge(moved_c[l][f], at(t, MOVED_C, C_T8T))
                    multiply(l, f, 1, t8t[f], right_side(l, f), D)

            def solve_off(t, l, halves=(0, 1)):
                for f in halves:
                    pe.wait_ge(moved_c[l][f], at(t, MOVED_C, C_Y))
                    multiply(l, f, 0, u8[f], y[f], D)

            def solve_last(t, l, halves=(0, 1)):
                for f in halves:
                    pe.wait_ge(moved_v[l][f], at(t, MOVED_V, V_R))
                    multiply(l, f, 1, t8t[f], right_side(l, f), D)

            def outputs(t, l):
                for f in range(2):
                    pe.wait_ge(moved_c[l][f], at(t, MOVED_C, C_Z))
                    pe.nop(nofuse=True)
                    for j in range(H // 2):
                        i, row = (H // 2 * f + j) // 2, D * (j % 2)
                        last = mm(bank(3)[row:row + D, P * i:P * (i + 1)], z[f][:, j, :], s_m[f][:, j, :],
                                  start=True, stop=True)
                last.then_inc(o_ready[l], 1)

            def project_out(t, l):
                if isinstance(t, int) and t + l == 0:
                    pe.wait_ge(late_landed, 16)
                pe.wait_ge(o_moved[l], at(t, 1, 1))
                for i in range(HP):
                    last = mm(bank(5, 0, P), o_t[:, i, :], mat(f"out{l}", i), start=(i == 0), stop=(i == HP - 1))
                last.then_inc(att_ready[l], 1)

            def feed_in(t):
                pe.wait_ge(norm_moved[2], t + 1)
                for n in range(FC):
                    last = mm(bank(VB, P * n, P * (n + 1)), mat("w1", n), normed_t[2], start=True, stop=True)
                last.then_inc(ff1_ready, 1)

            def feed_out(t):
                for n in range(FC):
                    pe.wait_ge(ff1_moved, at(t, FC, n + 1))
                    last = mm(bank(0, 0, P), ff[:, n, :], mat("w2", n), start=(n == 0), stop=(n == FC - 1))
                last.then_inc(ff2_ready, 1)

            def product_queries(t):
                pe.wait_ge(norm_moved[4], t + 1)
                for h in range(H):
                    last = mm(ps[:, P * h:P * (h + 1)], mat("wq", h), normed_t[4], start=True, stop=True)
                last.then_inc(qh_ready, 1)

            def key_products(t, q):
                c, lo = q // 2, 4 * (q % 2)
                pe.wait_ge(qh_moved, at(t, H, H))
                if q == 3:
                    pe.wait_ge(scores_used, at(t, 4, 1))
                for i in range(4):
                    h = lo + i
                    last = mm(bank(SCORE_BANK[q], P * i, P * (i + 1)), qh_t[D * c:D * (c + 1), h, :],
                              mat("keys", h)[D * c:D * (c + 1), :], start=True, stop=True)
                last.then_inc(scores_ready, 1)

            def up(t, m):
                pe.wait_ge(diag_ready, at(t, PARTS, m + 1))
                for k in range(SP):
                    s = SP * m + k
                    last = mm(bank(UP, 0, P), diag[:, m % 2, k, :], rows_got[:, s, P:2 * P],
                              start=(s == 0), stop=(s == SLOTS - 1))
                last.then_inc(up_done, 1)

            def turn_norm_4(t, f):
                if f is not None:
                    pe.wait_ge(ek_moved[0], at(f, 1, 1))
                turn_norm(t, 4)

            def up_first(c, d):
                if d is not None:
                    pe.wait_ge(out_ready, d + 1)
                up(c, 0)

            def turn_norm_3(m, f):
                if f is not None:
                    pe.wait_ge(ekc_moved[0], at(f, 2, 2))
                turn_norm(m, 3)

            def key_products_first(t, m):
                if m is not None:
                    pe.wait_ge(norm_moved[3], m + 1)
                key_products(t, 0)

            def keys_values_second(m, t):
                if t is not None:
                    pe.wait_ge(scores_used, at(t, 4, 4))
                keys_values(m, 1)

            def step(f, m, t, c, d):
                if t is not None:
                    key_scores(t, 1, None if m is None else (att_used, m + 1))
                if d is not None:
                    up(d, 3)
                if m is not None:
                    turn_norm(m, 2)
                if f is not None:
                    turn_norm(f, 0)
                if t is not None:
                    turn_blocks(t, 1)
                if m is not None:
                    feed_in(m)
                if t is not None:
                    blocks_2(t, 1)
                if f is not None:
                    project(f)
                if d is not None:
                    up(d, 4)
                if m is not None:
                    feed_out(m)
                if t is not None:
                    blocks_4(t, 1)
                if d is not None:
                    up(d, 5)
                if t is not None:
                    blocks_4_off(t, 1)
                if f is not None:
                    turn_norm(f, 1)
                    keys_values(f, 0)
                    queries(f, 0)
                if t is not None:
                    blocks_8(t, 1)
                    solve_first(t, 1)
                    solve_off(t, 1)
                    solve_last(t, 1)
                if f is not None:
                    turn_keys(f, 0)
                if t is not None:
                    outputs(t, 1)
                if f is not None:
                    turn_rest(f, 0)
                if t is not None:
                    project_out(t, 1)
                if f is not None:
                    key_scores(f, 0, None if t is None else (block_added, t + 1))
                if t is not None:
                    turn_norm_4(t, f)
                if m is not None:
                    turn_norm_3(m, f)
                if t is not None:
                    product_queries(t)
                if d is not None:
                    up(d, 6)
                if f is not None:
                    turn_blocks(f, 0)
                    blocks_2(f, 0)
                if t is not None:
                    key_products_first(t, m)
                    key_products(t, 1)
                    key_products(t, 2)
                if d is not None:
                    up(d, 7)
                if f is not None:
                    blocks_4(f, 0)
                if c is not None:
                    up_first(c, d)
                if f is not None:
                    blocks_4_off(f, 0)
                if t is not None:
                    key_products(t, 3)
                if f is not None:
                    blocks_8(f, 0)
                    solve_first(f, 0)
                if c is not None:
                    up(c, 1)
                if f is not None:
                    solve_off(f, 0)
                if m is not None:
                    keys_values_second(m, t)
                if f is not None:
                    solve_last(f, 0)
                if m is not None:
                    queries(m, 1)
                if f is not None:
                    outputs(f, 0)
                if m is not None:
                    turn_keys(m, 1)
                if f is not None:
                    project_out(f, 0)
                if m is not None:
                    turn_rest(m, 1)
                if c is not None:
                    up(c, 2)

            step(0, None, None, None, None)
            step(1, 0, None, None, None)
            step(2, 1, 0, None, None)
            step(3, 2, 1, 0, None)
            with pe.Fori(2, TILES - 2) as t:
                step(t + 2, t + 1, t, t - 1, t - 2)
            step(None, TILES - 1, TILES - 2, TILES - 3, TILES - 4)
            step(None, None, TILES - 1, TILES - 2, TILES - 3)
            for m in range(3, PARTS):
                up(TILES - 2, m)
            pe.wait_ge(out_ready, TILES - 1)
            for m in range(PARTS):
                up(TILES - 1, m)


def constants():
    i = np.arange(P)
    row, col = i[:, None], i[None, :]
    same = row // S == col // S

    def off_diagonal(n):
        return (row // (2 * n) == col // (2 * n)) & (row // n % 2 == 1) & (col // n % 2 == 0)

    f = np.concatenate([np.eye(P), off_diagonal(8).T, same & (row <= col), np.tile(np.arange(K), (P, 1))], axis=1)
    m = np.concatenate([off_diagonal(1).T, off_diagonal(2), off_diagonal(4)], axis=1)
    return f.astype(np.float32), m.astype(np.int32)


def kernel(x, L0_tok_weight, L0_tok_bias, L0_tok_mask, L0_attn_ip_w, L0_attn_ip_b, L0_attn_fw_ln_g, L0_attn_fw_ln_b,
           L0_attn_fw_slow_w, L0_attn_fw_out_w, L0_attn_ff_ln_g, L0_attn_ff_ln_b, L0_attn_ff_w1, L0_attn_ff_b1,
           L0_attn_ff_w2, L0_attn_ff_b2, L0_ffn_Wq, L0_ffn_bq, L0_ffn_keys, L0_ffn_w_down_embed, L0_ffn_w_up_embed):
    import concourse.bacc as bacc
    from concourse.bass_utils import run_bass_kernel_spmd

    def slow(w):
        w = np.asarray(w).reshape(H, 3 * D + 1, P)
        parts = [w[:, D * n:D * (n + 1)].reshape(H * D, P) for n in range(3)] + [w[:, 3 * D]]
        return np.concatenate(parts, axis=0).T

    def chunked(w):
        w = np.asarray(w)
        return w.reshape(w.shape[0], -1, P).transpose(2, 1, 0).reshape(P, -1)

    def column(v):
        return np.asarray(v).reshape(-1, P).T

    packed = np.concatenate([
        np.asarray(L0_attn_ip_w).T, slow(L0_attn_fw_slow_w[0]),
        column(L0_attn_fw_ln_g[0]), column(L0_attn_fw_ln_b[0]), column(L0_attn_fw_ln_g[1]), column(L0_attn_fw_ln_b[1]),
        column(L0_attn_ff_ln_g), column(L0_attn_ff_ln_b), column(L0_attn_ff_b1), column(L0_ffn_bq),
        chunked(L0_attn_fw_out_w[0]), np.asarray(L0_attn_ff_w1).T, chunked(L0_attn_ff_w2),
        slow(L0_attn_fw_slow_w[1]), chunked(L0_attn_fw_out_w[1]), np.asarray(L0_ffn_Wq).T,
        np.asarray(L0_ffn_keys).transpose(1, 3, 0, 2).reshape(P, H * P)], axis=1)
    assert packed.shape == (P, PACKED)
    fconst, iconst = constants()
    arrays = {
        "weight": np.asarray(L0_tok_weight),
        "x_t": np.asarray(x).T.reshape(GP, GC * B),
        "mask": np.asarray(L0_tok_mask),
        "packed": packed,
        "bias": np.asarray(L0_tok_bias),
        "rows": np.concatenate([np.asarray(L0_attn_ip_b), np.asarray(L0_attn_ff_b2)]),
        "fconst": fconst,
        "iconst": iconst,
        "table": np.concatenate([np.asarray(L0_ffn_w_down_embed), np.asarray(L0_ffn_w_up_embed)], axis=1),
    }
    nc = bacc.Bacc("TRN2", target_bir_lowering=False, num_devices=1)
    arrays = {k: np.ascontiguousarray(a) for k, a in arrays.items()}
    args = [nc.dram_tensor(k, a.shape, mybir.dt.from_np(a.dtype), kind="ExternalInput").ap() for k, a in arrays.items()]
    h_dram = nc.dram_tensor("h_dram", (B, S, P), F32, kind="Internal").ap()
    out = nc.dram_tensor("out", (B, S, P), F32, kind="ExternalOutput").ap()
    build(nc, *args, h_dram, out)
    r = run_bass_kernel_spmd(nc, [arrays], core_ids=[0])
    return r.results[0]["out"]
```
